# Optimizing a Trainium2 kernel written in Bass

```python
import numpy as np
import jax
import jax.numpy as jnp

def _softmax(x, axis=-1):
    return jax.nn.softmax(x, axis=axis)

def _gelu(x):
    return jax.nn.gelu(x, approximate=True)

def _silu(x):
    return jax.nn.silu(x)

def _sigmoid(x):
    return jax.nn.sigmoid(x)

def _layernorm(x, axis=-1, eps=1e-05):
    m = jnp.mean(x, axis=axis, keepdims=True)
    v = jnp.var(x, axis=axis, keepdims=True)
    return (x - m) / jnp.sqrt(v + eps)

def _scatter_add(tgt, idx, src, axis=0):
    return tgt.at[idx].add(src)

def _segment_sum(src, seg, n):
    return jax.ops.segment_sum(src, seg, n)
kernel_name = 'mk_seq_preln_d1_jaxref_r4_c894bc'

def setup_inputs(seed: int=0):
    np.random.seed(seed)
    _w = jnp.asarray

    def _L0_attn_setup():
        import jax, jax.numpy as jnp
        import numpy as np
        EMBD_DIM = 256
        NUM_HEADS = 16
        HEAD_DIM = EMBD_DIM // NUM_HEADS
        key = jax.random.key(seed)
        ks = jax.random.split(key, 9)
        B, S, D = (2, 512, EMBD_DIM)
        scale = 1.0 / np.sqrt(D)
        return {'x': jax.random.normal(ks[0], (B, S, D), dtype=jnp.float32), 'wq': jax.random.normal(ks[1], (D, D), dtype=jnp.float32) * scale, 'bq': jnp.zeros((D,), dtype=jnp.float32), 'wk': jax.random.normal(ks[2], (D, D), dtype=jnp.float32) * scale, 'bk': jnp.zeros((D,), dtype=jnp.float32), 'wv': jax.random.normal(ks[3], (D, D), dtype=jnp.float32) * scale, 'bv': jnp.zeros((D,), dtype=jnp.float32), 'wo': jax.random.normal(ks[4], (D, D), dtype=jnp.float32) * scale, 'bo': jnp.zeros((D,), dtype=jnp.float32)}
    _L0_attn_in = _L0_attn_setup()

    def _L0_ffn_setup():
        import jax, jax.numpy as jnp
        import numpy as np
        import math
        GOLDEN_CENTER = 1.0 / math.e
        GOLDEN_LOWER = 0.5 - math.log(4.0 / 3.0)
        GOLDEN_UPPER = 0.5
        B, T, D = (4, 512, 256)
        E = 8
        I = 1024 // (E // 2)

        def _routing_weights(x, Wr, temperature):
            inh = jax.nn.sigmoid(x @ Wr / temperature)
            in_zone = (inh >= GOLDEN_LOWER) & (inh <= GOLDEN_UPPER)
            dist = jnp.abs(inh - GOLDEN_CENTER)
            w = jnp.exp(-dist / 0.1) * in_zone.astype(x.dtype)
            wsum = w.sum(axis=-1, keepdims=True)
            no_expert = wsum < 1e-08
            fb = jnp.exp(-dist / 0.3)
            _, top2 = jax.lax.top_k(fb, 2)
            fb_mask = jax.nn.one_hot(top2, E, dtype=x.dtype).sum(axis=-2)
            fb_w = fb * fb_mask
            fb_w = fb_w / jnp.clip(fb_w.sum(axis=-1, keepdims=True), 1e-08)
            w = jnp.where(no_expert, fb_w, w)
            wsum = w.sum(axis=-1, keepdims=True)
            return w / jnp.clip(wsum, 1e-08)
        key = jax.random.key(seed)
        k = jax.random.split(key, 6)
        s_d = 1.0 / math.sqrt(D)
        s_i = 1.0 / math.sqrt(I)
        return {'x': jax.random.normal(k[0], (B, T, D), jnp.float32), 'Wg': jax.random.normal(k[1], (E, D, I), jnp.float32) * s_d, 'Wu': jax.random.normal(k[2], (E, D, I), jnp.float32) * s_d, 'Wd': jax.random.normal(k[3], (E, I, D), jnp.float32) * s_i, 'Wr': jax.random.normal(k[4], (D, E), jnp.float32) * s_d, 'temperature': jnp.ones((1,), jnp.float32)}
    _L0_ffn_in = _L0_ffn_setup()
    _d = {'L0_attn_x': _L0_attn_in['x'], 'L0_attn_wq': _L0_attn_in['wq'], 'L0_attn_bq': _L0_attn_in['bq'], 'L0_attn_wk': _L0_attn_in['wk'], 'L0_attn_bk': _L0_attn_in['bk'], 'L0_attn_wv': _L0_attn_in['wv'], 'L0_attn_bv': _L0_attn_in['bv'], 'L0_attn_wo': _L0_attn_in['wo'], 'L0_attn_bo': _L0_attn_in['bo'], 'L0_ffn_Wg': _L0_ffn_in['Wg'], 'L0_ffn_Wu': _L0_ffn_in['Wu'], 'L0_ffn_Wd': _L0_ffn_in['Wd'], 'L0_ffn_Wr': _L0_ffn_in['Wr'], 'L0_ffn_temperature': _L0_ffn_in['temperature']}
    _x0 = _d['L0_attn_x']
    _d['L0_attn_x'] = jax.random.normal(jax.random.fold_in(jax.random.key(seed), 1), (4, 2048, 256), dtype=_x0.dtype)
    del _x0
    return _d

def reference(L0_attn_x, L0_attn_wq, L0_attn_bq, L0_attn_wk, L0_attn_bk, L0_attn_wv, L0_attn_bv, L0_attn_wo, L0_attn_bo, L0_ffn_Wg, L0_ffn_Wu, L0_ffn_Wd, L0_ffn_Wr, L0_ffn_temperature):

    def _L0_attn_ref(x, wq, bq, wk, bk, wv, bv, wo, bo):
        import jax, jax.numpy as jnp
        import numpy as np
        EMBD_DIM = 256
        NUM_HEADS = 16
        HEAD_DIM = EMBD_DIM // NUM_HEADS
        B, S, D = x.shape
        H, hd = (NUM_HEADS, HEAD_DIM)
        q = (x @ wq + bq).reshape(B, S, H, hd).transpose(0, 2, 1, 3)
        k = (x @ wk + bk).reshape(B, S, H, hd).transpose(0, 2, 1, 3)
        v = (x @ wv + bv).reshape(B, S, H, hd).transpose(0, 2, 1, 3)
        scores = jnp.einsum('bhqd,bhkd->bhqk', q, k) / jnp.sqrt(jnp.float32(hd))
        causal = jnp.tril(jnp.ones((S, S), dtype=bool))
        neg = jnp.finfo(scores.dtype).min
        scores = jnp.where(causal[None, None, :, :], scores, neg)
        attn = jax.nn.softmax(scores, axis=-1)
        out = jnp.einsum('bhqk,bhkd->bhqd', attn, v)
        out = out.transpose(0, 2, 1, 3).reshape(B, S, D)
        return out @ wo + bo

    def _L0_ffn_ref(x, Wg, Wu, Wd, Wr, temperature):
        import jax, jax.numpy as jnp
        import numpy as np
        import math
        GOLDEN_CENTER = 1.0 / math.e
        GOLDEN_LOWER = 0.5 - math.log(4.0 / 3.0)
        GOLDEN_UPPER = 0.5
        B, T, D = (4, 512, 256)
        E = 8
        I = 1024 // (E // 2)

        def _routing_weights(x, Wr, temperature):
            inh = jax.nn.sigmoid(x @ Wr / temperature)
            in_zone = (inh >= GOLDEN_LOWER) & (inh <= GOLDEN_UPPER)
            dist = jnp.abs(inh - GOLDEN_CENTER)
            w = jnp.exp(-dist / 0.1) * in_zone.astype(x.dtype)
            wsum = w.sum(axis=-1, keepdims=True)
            no_expert = wsum < 1e-08
            fb = jnp.exp(-dist / 0.3)
            _, top2 = jax.lax.top_k(fb, 2)
            fb_mask = jax.nn.one_hot(top2, E, dtype=x.dtype).sum(axis=-2)
            fb_w = fb * fb_mask
            fb_w = fb_w / jnp.clip(fb_w.sum(axis=-1, keepdims=True), 1e-08)
            w = jnp.where(no_expert, fb_w, w)
            wsum = w.sum(axis=-1, keepdims=True)
            return w / jnp.clip(wsum, 1e-08)
        weights = _routing_weights(x, Wr, temperature)
        gate = jnp.einsum('btd,edi->beti', x, Wg)
        up = jnp.einsum('btd,edi->beti', x, Wu)
        h = jax.nn.silu(gate) * up
        e_out = jnp.einsum('beti,eid->betd', h, Wd)
        out = jnp.einsum('bte,betd->btd', weights, e_out)
        return out
    x = L0_attn_x
    x = x + _L0_attn_ref(_layernorm(x, axis=-1), L0_attn_wq, L0_attn_bq, L0_attn_wk, L0_attn_bk, L0_attn_wv, L0_attn_bv, L0_attn_wo, L0_attn_bo)
    x = x + _L0_ffn_ref(_layernorm(x, axis=-1), L0_ffn_Wg, L0_ffn_Wu, L0_ffn_Wd, L0_ffn_Wr, L0_ffn_temperature)
    return x

_drawn_inputs = setup_inputs


def setup_inputs(seed=0):
    import zlib

    import numpy as np

    out = dict(_drawn_inputs(seed))
    spreads = {'L0_attn_bq': (0.0, 0.295),
     'L0_attn_bk': (0.0, 0.8),
     'L0_attn_bv': (0.0, 0.1),
     'L0_attn_bo': (0.0, 0.1)}
    factors = {}
    for name, (base, spread) in spreads.items():
        noise = np.random.default_rng([zlib.crc32(name.encode()), seed]).standard_normal(out[name].shape)
        drawn = base * np.exp(spread * noise) if base else spread * noise
        out[name] = jnp.asarray(drawn.astype(out[name].dtype))
    for name, factor in factors.items():
        out[name] = (out[name] * factor).astype(out[name].dtype)
    return out
```

```python
import math
from contextlib import ExitStack

import concourse.bass as bass
from concourse import mybir

F32 = mybir.dt.float32
F32R = mybir.dt.float32r
ALU = mybir.AluOpType
ACT = mybir.ActivationFunctionType
AX_X = mybir.AxisListType.X

P = 128
B, S, D = 4, 2048, 256
H, HD = 16, 16
E, I = 8, 256
KT = D // P
TILE = 512
BLOCKS = TILE // P
TILES_B = S // TILE
TILES = B * TILES_B
G = 4
GROUPS_B = H // G
GROUPS = B * GROUPS_B
VW = 2 * HD
EPS = 1e-5
LOW = -3.0e38


def wait_apart(engine, sem, value, passed):
    engine.wait_ge(sem, value)
    engine.sem_inc(passed, 1)


class Tally:

    def __init__(self, sem, per_tile):
        self.sem, self.per_tile, self.count = sem, per_tile, 0

    def start(self):
        self.count = 0

    def up(self, instruction):
        instruction.then_inc(self.sem, 1)
        self.count += 1

    def wait(self, engine, tile):
        engine.wait_ge(self.sem, tile * self.per_tile + self.count)

    def end(self):
        assert self.count == self.per_tile, (self.count, self.per_tile)


def layer_norm(dve, chain, tile, passed, x, stats, moments, small, xn, var_ready, std_ready, xn_ready):
    for j in range(BLOCKS):
        chain.up(dve.bn_stats(stats[:, j, :], x[:, j, :]))
    wait_apart(dve, chain.sem, tile * chain.per_tile + chain.count, passed)
    for j in range(BLOCKS):
        chain.up(dve.bn_aggr(moments[:, j, :], stats[:, j, :]))
    chain.wait(dve, tile)
    var, std, rec, tmp = (small[:, n, :] for n in range(4))
    dve.tensor_scalar(var, moments[:, :, 1], EPS, None, ALU.add).then_inc(var_ready, 1)
    dve.wait_ge(var_ready, tile + 1)
    dve.wait_ge(std_ready, tile + 1)
    chain.up(dve.reciprocal(rec, std))
    chain.wait(dve, tile)
    chain.up(dve.tensor_tensor(tmp, var, rec, ALU.mult))
    chain.wait(dve, tile)
    chain.up(dve.tensor_tensor(std, std, tmp, ALU.add))
    chain.wait(dve, tile)
    chain.up(dve.tensor_scalar(tmp, std, 0.5, None, ALU.mult))
    chain.wait(dve, tile)
    chain.up(dve.reciprocal(rec, tmp))
    chain.wait(dve, tile)
    for j in range(BLOCKS):
        dve.tensor_scalar(xn[:, j, :], x[:, j, :], moments[:, j, 0:1], rec[:, j:j + 1],
                          ALU.subtract, ALU.mult).then_inc(xn_ready, 1)


LN_CHAIN = 4 + 4 + 5


def project(nc, ident, x_in, wq, bq, wk, bk, wv, bv, q_hi, q_lo, k_hi, k_lo, v_all):
    with ExitStack() as ctx:
        def sb(name, shape, dt=F32):
            return ctx.enter_context(nc.sbuf_tensor("pr_" + name, shape, dt))

        def sem(name):
            return ctx.enter_context(nc.semaphore("pr_" + name))

        w_sb = sb("w", [P, 3, KT, D])
        bias_col = sb("bias_col", [P, 2, KT])
        bv_row = sb("bv_row", [P, 2, D])
        x_t = [sb(f"x{k}", [P, BLOCKS, D]) for k in range(2)]
        stats = sb("stats", [P, BLOCKS, 6])
        moments = sb("moments", [P, BLOCKS, 2])
        small = sb("small", [P, 4, BLOCKS])
        xn = [sb(f"xn{k}", [P, BLOCKS, D]) for k in range(2)]
        xnT = [sb(f"xnT{k}", [P, KT, TILE]) for k in range(2)]
        qk_f = [sb(f"qk_f{k}", [P, 2 * KT, TILE]) for k in range(2)]
        qk_h = [sb(f"qk_h{k}", [P, 2 * KT, TILE], F32R) for k in range(2)]
        qk_l = [sb(f"qk_l{k}", [P, 2 * KT, TILE], F32R) for k in range(2)]
        v_t = [sb(f"v{k}", [P, BLOCKS, H, VW]) for k in range(2)]
        ps_T = [ctx.enter_context(nc.psum_tensor(f"pr_psT{m}", [P, TILE], F32)) for m in range(KT)]
        ps_qk = [ctx.enter_context(nc.psum_tensor(f"pr_psqk{m}", [P, TILE], F32)) for m in range(4)]
        ps_v = [ctx.enter_context(nc.psum_tensor(f"pr_psv{m}", [P, 2, D], F32)) for m in range(2)]

        consts = sem("consts_landed")
        ones = sem("v_ones")
        x_landed = [sem(f"x_landed{k}") for k in range(2)]
        chain_sem = sem("ln_chain")
        passed = sem("passed")
        var_ready, std_ready, xn_ready = sem("var_ready"), sem("std_ready"), sem("xn_ready")
        xT_psum = sem("xT_psum")
        xT_ready = sem("xT_ready")
        qk_psum = sem("qk_psum")
        v_psum = sem("v_psum")
        qk_full = sem("qk_full")
        hi_ready = sem("hi_ready")
        lo_ready = sem("lo_ready")
        v_ready = sem("v_ready")
        stored = [sem(f"stored{k}") for k in range(2)]

        STORES = 4 + BLOCKS
        block = ctx.enter_context(nc.Block())

        @block.sync
        def _(sp):
            for n, w in enumerate((wq, wk, wv)):
                sp.dma_start(w_sb[:, n], w.rearrange("(k p) n -> p k n", p=P)).then_inc(consts, 16)
            for n, bias in enumerate((bq, bk)):
                sp.dma_start(bias_col[:, n], bias.rearrange("(k p) -> p k", p=P),
                             allow_slow_non_contiguous=True).then_inc(consts, 16)
            for n in range(2):
                sp.dma_start(bv_row[:, n], bv.rearrange("(a n) -> a n", a=1).to_broadcast([P, D])).then_inc(consts, 16)
            for k in range(2):
                sp.sem_inc(stored[k], 16 * STORES)
                sp.dma_start(x_t[k][:], x_in[k * TILE:(k + 1) * TILE, :].rearrange(
                    "(j p) d -> p j d", p=P)).then_inc(x_landed[k], 16)

            def store(b, t, j, k):
                sp.wait_ge(lo_ready, t * 4 + 4)
                sp.wait_ge(v_ready, t * 2 + 4)
                rows, cols = bass.ds(b * D, D), bass.ds(j * (2 * TILE) + k * TILE, TILE)
                for dram, tile, m in ((q_hi, qk_h, 0), (q_lo, qk_l, 0), (k_hi, qk_h, 2), (k_lo, qk_l, 2)):
                    sp.dma_start(dram[rows, cols].rearrange("(m p) n -> p m n", p=P),
                                 tile[k][:, m:m + 2].bitcast(F32)).then_inc(stored[k], 16)
                for i in range(BLOCKS):
                    sp.dma_start(
                        v_all[bass.ds(b * GROUPS_B, GROUPS_B),
                              bass.ds(j * (2 * TILE) + (k * TILE + i * P), P), :].rearrange("g p n -> p g n"),
                        v_t[k][:, i].rearrange("p (g h) n -> p g (h n)", h=G)).then_inc(stored[k], 16)

            def pair(b, j, load):
                for k in range(2):
                    t = b * TILES_B + j * 2 + k
                    if load:
                        sp.wait_ge(xn_ready, t * BLOCKS + BLOCKS)
                        sp.dma_start(x_t[k][:], x_in[bass.ds(b * S + j * (2 * TILE) + (k + 2) * TILE, TILE), :].rearrange(
                            "(j p) d -> p j d", p=P)).then_inc(x_landed[k], 16)
                    store(b, t, j, k)

            with sp.Fori(0, B - 1) as b:
                with sp.Fori(0, TILES_B // 2) as j:
                    pair(b, j, True)
            for j in range(TILES_B // 2):
                pair(B - 1, j, j < TILES_B // 2 - 1)
            for k in range(2):
                sp.wait_ge(stored[k], 16 * STORES * (TILES // 2 + 1))

        @block.gpsimd
        def _(pool):
            for k in range(2):
                pool.memset(v_t[k][:], 1.0).then_inc(ones, 1)
            with pool.Fori(0, B) as b:
                with pool.Fori(0, TILES_B // 2) as j:
                    for k in range(2):
                        t = b * TILES_B + j * 2 + k
                        n = b * (TILES_B // 2) + j
                        pool.wait_ge(stored[k], n * (16 * STORES) + 16 * STORES)
                        for m in range(4):
                            pool.wait_ge(hi_ready, t * 4 + m + 1)
                            pool.tensor_tensor(qk_l[k][:, m], qk_f[k][:, m], qk_h[k][:, m].bitcast(F32),
                                               ALU.subtract).then_inc(lo_ready, 1)

        @block.scalar
        def _(act):
            act.sem_inc(qk_full, 4)
            act.wait_ge(consts, 16 * 7)
            with act.Fori(0, TILES // 2) as it:
                for k in range(2):
                    t = it * 2 + k
                    act.wait_ge(var_ready, t + 1)
                    act.activation(small[:, 1, :], small[:, 0, :], ACT.Sqrt).then_inc(std_ready, 1)
                    for m in range(KT):
                        act.wait_ge(xT_psum, t * KT + m + 1)
                        act.activation(xnT[k][:, m], ps_T[m][:], ACT.Identity).then_inc(xT_ready, 1)
                    act.wait_ge(stored[k], it * (16 * STORES) + 16 * STORES)
                    for m in range(4):
                        act.wait_ge(qk_psum, t * 4 + m + 1)
                        act.activation(qk_f[k][:, m], ps_qk[m][:], ACT.Identity,
                                       bias=bias_col[:, m // 2, m % 2:m % 2 + 1]).then_inc(qk_full, 1)

        @block.vector
        def _(dve):
            chain = Tally(chain_sem, LN_CHAIN)
            dve.sem_inc(v_ready, 2)
            dve.wait_ge(consts, 16 * 7)
            dve.wait_ge(ones, 2)
            with dve.Fori(0, TILES // 2) as it:
                for k in range(2):
                    t = it * 2 + k
                    dve.wait_ge(x_landed[k], it * 16 + 16)
                    chain.start()
                    layer_norm(dve, chain, t, passed, x_t[k], stats, moments, small, xn[k],
                               var_ready, std_ready, xn_ready)
                    chain.end()
                    dve.wait_ge(stored[k], it * (16 * STORES) + 16 * STORES)
                    for m in range(4):
                        dve.wait_ge(qk_full, t * 4 + m + 5)
                        dve.tensor_copy(qk_h[k][:, m], qk_f[k][:, m]).then_inc(hi_ready, 1)
                    for m in range(2):
                        dve.wait_ge(v_psum, t * 2 + m + 1)
                        dve.tensor_tensor(
                            v_t[k][:, 2 * m:2 * m + 2, :, 0:HD].rearrange("p j h c -> p (j h) c"),
                            ps_v[m][:].rearrange("p j (h c) -> p (j h) c", c=HD),
                            bv_row[:].rearrange("p j (h c) -> p (j h) c", c=HD), ALU.add).then_inc(v_ready, 1)

        @block.tensor
        def _(pe):
            pe.wait_ge(consts, 16 * 7)
            with pe.Fori(0, TILES // 2) as it:
                for k in range(2):
                    t = it * 2 + k
                    pe.wait_ge(xn_ready, t * BLOCKS + BLOCKS)
                    for m in range(KT):
                        for j in range(BLOCKS):
                            ins = pe.transpose(ps_T[m][:, j * P:(j + 1) * P], xn[k][:, j, m * P:(m + 1) * P], ident[:])
                        ins.then_inc(xT_psum, 1)
                    pe.wait_ge(xT_ready, t * KT + KT)
                    for m in range(4):
                        pe.wait_ge(qk_full, t * 4 + m + 1)
                        for c in range(KT):
                            ins = pe.matmul(ps_qk[m][:], w_sb[:, m // 2, c, (m % 2) * P:(m % 2 + 1) * P],
                                            xnT[k][:, c], start=(c == 0), stop=(c == KT - 1))
                        ins.then_inc(qk_psum, 1)
                    for m in range(2):
                        pe.wait_ge(v_ready, t * 2 + m + 1)
                        for j in range(2):
                            for c in range(KT):
                                ins = pe.matmul(ps_v[m][:, j], xnT[k][:, c, (2 * m + j) * P:(2 * m + j + 1) * P],
                                                w_sb[:, 2, c], start=(c == 0), stop=(c == KT - 1))
                        ins.then_inc(v_psum, 1)


UNITS = [(j, kb, max(0, kb - BLOCKS * j) * P) for j in reversed(range(TILES_B)) for kb in range(BLOCKS * (j + 1))]
LAST = {max(u for u, x in enumerate(UNITS) if x[0] == j): j for j in range(TILES_B)}
NU = len(UNITS)
AHEAD = 2
RING = 4
QB = S // P
CHUNKS = [(i, c, h, TILE if c < i // BLOCKS else (i % BLOCKS + 1) * P)
          for i in range(QB) for c in range(i // BLOCKS + 1) for h in range(G)]
NC = len(CHUNKS)
KMAX = 4 * HD + 1
KSCORE = 4 * HD + 3
MX_FROM, MX_TO = 4, 33


def chunk_plan():
    width = [TILE - u[2] for u in UNITS]
    total, plan, done = sum(width[MX_FROM:MX_TO]), [], 0
    for u in range(NU):
        part = sum(width[MX_FROM:u + 1]) if u >= MX_FROM else 0
        upto = NC if u >= MX_TO - 1 else NC * part // total
        plan.append(range(done, upto))
        done = upto
    return plan


def attend(nc, ident, q_hi, q_lo, k_hi, k_lo, v_all, m_all, o_all):
    with ExitStack() as ctx:
        def sb(name, shape, dt=F32):
            return ctx.enter_context(nc.sbuf_tensor("at_" + name, shape, dt))

        def sem(name):
            return ctx.enter_context(nc.semaphore("at_" + name))

        q_st = [sb(f"q{k}", [KSCORE, G, S], F32R) for k in range(2)]
        k_st = [sb(f"k{k}", [KSCORE, G, S], F32R) for k in range(2)]
        v_st = [sb(f"v{k}", [P, QB, G * VW]) for k in range(2)]
        probs = [sb(f"probs{r}", [P, G, TILE]) for r in range(RING)]
        mask = sb("mask", [P, TILE])
        part = sb("part", [P, QB, G, TILES_B])
        row_max = sb("row_max", [P, G, QB])
        max_h = sb("max_h", [P, G * QB], F32R)
        neg_max = sb("neg_max", [P, 2, G * QB])
        max_rows = sb("max_rows", [P, P], F32R)
        o_sb = [sb(f"o{k}", [P, TILE]) for k in range(2)]
        ps_s = [ctx.enter_context(nc.psum_tensor(f"at_pss{m}", [P, 2, TILE], F32)) for m in range(2)]
        ps_m = [ctx.enter_context(nc.psum_tensor(f"at_psm{m}", [P, TILE], F32)) for m in range(2)]
        ps_o = [ctx.enter_context(nc.psum_tensor(f"at_pso{m}", [P, TILE], F32)) for m in range(2)]

        mask_zero = sem("mask_zero")
        passed_dve, passed_pool, passed_sp = sem("passed_dve"), sem("passed_pool"), sem("passed_sp")
        init = sem("init")
        landed = [[sem(f"landed{k}{c}") for c in range(TILES_B)] for k in range(2)]
        v_landed = [sem(f"v_landed{k}") for k in range(2)]
        chunk_psum = sem("chunk_psum")
        chunk_max = sem("chunk_max")
        max_step = sem("max_step")
        rows_psum = sem("rows_psum")
        rows_ready = sem("rows_ready")
        rows_saved = sem("rows_saved")
        rows_landed = sem("rows_landed")
        score_psum = sem("score_psum")
        exp_ready = sem("exp_ready")
        masked = sem("masked")
        unit_done = sem("unit_done")
        o_ready = sem("o_ready")
        o_stored = [sem(f"o_stored{k}") for k in range(2)]

        block = ctx.enter_context(nc.Block())
        QUARTER = 8 * 16
        MAX_STEPS = 4

        def load_quarter(sp, n, k, c):
            cols = slice(c * TILE, (c + 1) * TILE)
            rows = bass.ds(n * (G * HD), G * HD)
            for stack, halves in ((q_st[k], (q_hi, q_hi, q_lo, q_lo)), (k_st[k], (k_hi, k_lo, k_hi, k_lo))):
                for slot, dram in enumerate(halves):
                    sp.dma_start(stack[slot * HD:(slot + 1) * HD, :, cols].bitcast(F32),
                                 dram[rows, cols].rearrange("(h r) n -> r h n", r=HD)).then_inc(landed[k][c], 16)

        def load_v(sp, n, k):
            for c in range(TILES_B):
                sp.dma_start(v_st[k][:, c * BLOCKS:(c + 1) * BLOCKS],
                             v_all[bass.ds(n, 1), c * TILE:(c + 1) * TILE, :].rearrange(
                                 "a (i p) n -> p (a i) n", p=P)).then_inc(v_landed[k], 16)

        @block.sync
        def _(sp):
            def store_maxima(n, k):
                sp.wait_ge(rows_ready, n + 1)
                sp.dma_start(m_all[bass.ds(n * P, P), :], max_rows[:].bitcast(F32)).then_inc(rows_saved, 16)
                sp.wait_ge(rows_saved, n * 16 + 16)
                sp.dma_start(q_st[k][KMAX:KSCORE].bitcast(F32),
                             m_all[bass.ds(n * P, P), :].rearrange("(a h i) n -> a h (i n)", a=2, h=G)).then_inc(rows_landed, 16)

            def group(n, k, load=True, after=True):
                for c in reversed(range(TILES_B)):
                    last = max(u for u, x in enumerate(UNITS) if x[0] == c)
                    if load:
                        wait_apart(sp, score_psum, n * (2 * NU) + 2 * (last + 1), passed_sp)
                        load_quarter(sp, n + 2, k, c)
                    if after and c == 1:
                        store_maxima(n + 1, 1 - k)
                    wait_apart(sp, o_ready, n * TILES_B + (TILES_B - c + 2), passed_sp)
                    sp.dma_start(o_all[bass.ds(n * P, P), c * TILE:(c + 1) * TILE], o_sb[c % 2][:]).then_inc(o_stored[c % 2], 16)
                if load:
                    load_v(sp, n + 2, k)

            sp.wait_ge(init, 6)
            for n in range(2):
                for c in range(TILES_B):
                    load_quarter(sp, n, n, c)
                load_v(sp, n, n)
            store_maxima(0, 0)
            with sp.Fori(0, GROUPS // 2 - 1) as it:
                for k in range(2):
                    group(it * 2 + k, k)
            group(GROUPS - 2, 0, load=False)
            group(GROUPS - 1, 1, load=False, after=False)
            for k in range(2):
                sp.wait_ge(o_stored[k], 16 * (2 * GROUPS + 1))

        @block.gpsimd
        def _(pool):
            pool.memset(mask[:], 0.0).then_inc(mask_zero, 1)
            pool.wait_ge(mask_zero, 1)
            pool.affine_select(out=mask[:, TILE - P:], in_=mask[:, TILE - P:], compare_op=ALU.is_ge, fill=LOW,
                               base=0, pattern=[[-1, P]], channel_multiplier=1).then_inc(init, 1)
            with pool.Fori(0, GROUPS) as n:
                for u, (j, kb, first) in enumerate(UNITS):
                    if kb < BLOCKS * j:
                        continue
                    wait_apart(pool, exp_ready, n * (2 * NU) + 2 * (u + 1), passed_pool)
                    diagonal = probs[u % RING][:, :, first:first + P]
                    pool.affine_select(out=diagonal, in_=diagonal, compare_op=ALU.is_ge, fill=0.0, base=0,
                                       pattern=[[0, G], [1, P]], channel_multiplier=-1).then_inc(masked, 1)

        @block.scalar
        def _(act):
            def exponentials(n, u):
                _, _, first = UNITS[u]
                for half in range(2):
                    act.wait_ge(score_psum, n * (2 * NU) + 2 * u + half + 1)
                    act.activation(probs[u % RING][:, 2 * half:2 * half + 2, first:], ps_s[half][:, :, first:],
                                   ACT.Exp, scale=HD ** -0.5).then_inc(exp_ready, 1)

            def group(n, after=True):
                for u in range(NU):
                    if u + AHEAD < NU:
                        exponentials(n, u + AHEAD)
                    elif after:
                        exponentials(n + 1, u + AHEAD - NU)
                    if u in LAST:
                        j = LAST[u]
                        act.wait_ge(unit_done, n * NU + u + 1)
                        act.wait_ge(o_stored[j % 2], n * 32 + 16 * ((TILES_B - 1 - j) // 2 + 1))
                        act.activation(o_sb[j % 2][:], ps_o[j % 2][:], ACT.Copy).then_inc(o_ready, 1)

            act.sem_inc(o_ready, 2)
            for k in range(2):
                act.sem_inc(o_stored[k], 16)
            for u in range(AHEAD):
                exponentials(0, u)
            with act.Fori(0, GROUPS - 1) as n:
                group(n)
            group(GROUPS - 1, after=False)

        @block.vector
        def _(dve):
            dve.sem_inc(rows_landed, 16)
            dve.memset(part[:], LOW).then_inc(init, 1)
            for k in range(2):
                dve.memset(q_st[k][4 * HD:, :, :].bitcast(F32), 0.0).then_inc(init, 1)
                dve.memset(k_st[k][4 * HD:, :, :].bitcast(F32), 1.0).then_inc(init, 1)
            dve.wait_ge(init, 6)
            with dve.Fori(0, GROUPS) as n:
                for x, (i, c, h, width) in enumerate(CHUNKS):
                    wait_apart(dve, chunk_psum, n * NC + x + 1, passed_dve)
                    scores = ps_m[x % 2][:, 0:width]
                    if c < i // BLOCKS:
                        dve.tensor_reduce(part[:, i, h, c:c + 1], scores, AX_X, ALU.max).then_inc(chunk_max, 1)
                    else:
                        dve.tensor_tensor_reduce(scores, scores, mask[:, TILE - width:], 1.0, LOW, ALU.add,
                                                 ALU.max, part[:, i, h, c:c + 1]).then_inc(chunk_max, 1)
                dve.wait_ge(chunk_max, n * NC + NC)
                dve.tensor_reduce(row_max[:].rearrange("p h i -> p i h"), part[:], AX_X, ALU.max).then_inc(max_step, 1)
                dve.wait_ge(max_step, n * MAX_STEPS + 1)
                row = row_max[:].rearrange("p h i -> p (h i)")
                dve.tensor_scalar(max_h[:], row, -1.0, None, ALU.mult).then_inc(max_step, 1)
                dve.wait_ge(max_step, n * MAX_STEPS + 2)
                dve.tensor_copy(neg_max[:, 0], max_h[:].bitcast(F32)).then_inc(max_step, 1)
                dve.scalar_tensor_tensor(out=neg_max[:, 1], in0=row, scalar=-1.0, in1=max_h[:].bitcast(F32),
                                         op0=ALU.mult, op1=ALU.subtract).then_inc(max_step, 1)
                dve.wait_ge(rows_psum, n + 1)
                dve.wait_ge(rows_landed, n * 16 + 16)
                dve.tensor_copy(max_rows[:], ps_m[0][:, 0:P]).then_inc(rows_ready, 1)

        @block.tensor
        def _(pe):
            def scores(n, k, u, very_first=False):
                j, kb, first = UNITS[u]
                for half in range(2):
                    if not very_first:
                        pe.wait_ge(exp_ready, n * (2 * NU) + (2 * u - 1 + half))
                    for h in (2 * half, 2 * half + 1):
                        ins = pe.matmul(ps_s[half][:, h % 2, first:], k_st[k][:, h, kb * P:(kb + 1) * P],
                                        q_st[k][:, h, j * TILE + first:(j + 1) * TILE], start=True, stop=True)
                    ins.then_inc(score_psum, 1)

            def chunk(n, k, pair, x):
                i, c, h, width = CHUNKS[x]
                if c == 0 and h == 0 and i % BLOCKS == 0:
                    pe.wait_ge(landed[k][i // BLOCKS], pair * QUARTER + QUARTER)
                if x == 0 and not (isinstance(n, int) and n == 0):
                    pe.wait_ge(rows_ready, n)
                if x >= 2:
                    pe.wait_ge(chunk_max, n * NC + (x - 1))
                pe.matmul(ps_m[x % 2][:, 0:width], q_st[k][0:KMAX, h, i * P:(i + 1) * P],
                          k_st[k][0:KMAX, h, c * TILE:c * TILE + width], start=True, stop=True).then_inc(chunk_psum, 1)

            def max_to_rows(n):
                pe.wait_ge(max_step, n * MAX_STEPS + MAX_STEPS)
                pe.transpose(ps_m[0][:, 0:P], neg_max[:].rearrange("p a n -> p (a n)"), ident[:]).then_inc(rows_psum, 1)

            def times_v(n, k, pair, u):
                j, kb, first = UNITS[u]
                if u == 0:
                    pe.wait_ge(v_landed[k], pair * (16 * TILES_B) + 16 * TILES_B)
                if kb == 0:
                    pe.wait_ge(o_ready, n * TILES_B + (TILES_B - j))
                if kb >= BLOCKS * j:
                    pe.wait_ge(masked, n * (TILES_B * BLOCKS) + (TILES_B - 1 - j) * BLOCKS + kb - BLOCKS * j + 1)
                else:
                    pe.wait_ge(exp_ready, n * (2 * NU) + 2 * (u + 1))
                for h in range(G):
                    ins = pe.matmul(ps_o[j % 2][h * VW:(h + 1) * VW, first:], v_st[k][:, kb, h * VW:(h + 1) * VW],
                                    probs[u % RING][:, h, first:], start=kb == 0, stop=u in LAST)
                ins.then_inc(unit_done, 1)

            plan = chunk_plan()

            def group(n, k, pair, after=True):
                next_pair = pair + k
                for u in range(NU):
                    if u + AHEAD < NU:
                        scores(n, k, u + AHEAD)
                    elif after:
                        if u + AHEAD == NU:
                            pe.wait_ge(rows_landed, n * 16 + 48)
                        scores(n + 1, 1 - k, u + AHEAD - NU)
                    if after:
                        for x in plan[u]:
                            chunk(n + 1, 1 - k, next_pair, x)
                        if u == MX_TO:
                            max_to_rows(n + 1)
                    times_v(n, k, pair, u)

            pe.wait_ge(init, 6)
            for x in range(NC):
                chunk(0, 0, 0, x)
            max_to_rows(0)
            pe.wait_ge(rows_landed, 32)
            for u in range(AHEAD):
                scores(0, 0, u, very_first=u == 0)
            with pe.Fori(0, GROUPS // 2 - 1) as it:
                for k in range(2):
                    group(it * 2 + k, k, it)
            group(GROUPS - 2, 0, GROUPS // 2 - 1)
            group(GROUPS - 1, 1, GROUPS // 2 - 1, after=False)


CENTER = 1.0 / math.e
LOWER = 0.5 - math.log(4.0 / 3.0)
UPPER = 0.5


def route(nc, ident, x_in, o_all, wo, bo, wr, temperature, x1_all, x2T_all, w_all):
    with ExitStack() as ctx:
        def sb(name, shape, dt=F32):
            return ctx.enter_context(nc.sbuf_tensor("ro_" + name, shape, dt))

        def sem(name):
            return ctx.enter_context(nc.semaphore("ro_" + name))

        wo_sb = sb("wo", [P, KT, D])
        bo_row = sb("bo", [P, D])
        wr_sb = sb("wr", [P, KT, E])
        temp = sb("temp", [P, 1])
        temp_r = sb("temp_r", [P, 1])
        num = sb("num", [P, KT, S])
        den = sb("den", [P, KT, S])
        att = sb("att", [P, KT, S])
        x_t = [sb(f"x{k}", [P, BLOCKS, D]) for k in range(2)]
        xb = [sb(f"xb{k}", [P, BLOCKS, D]) for k in range(2)]
        x1 = [sb(f"x1{k}", [P, BLOCKS, D]) for k in range(2)]
        stats = sb("stats", [P, BLOCKS, 6])
        moments = sb("moments", [P, BLOCKS, 2])
        small = sb("small", [P, 4, BLOCKS])
        x2 = [sb(f"x2{k}", [P, BLOCKS, D]) for k in range(2)]
        x2T = [sb(f"x2T{k}", [P, KT, TILE]) for k in range(2)]
        NB = TILES * BLOCKS
        logits = sb("logits", [P, NB, E])
        ps_y = [ctx.enter_context(nc.psum_tensor(f"ro_psy{m}", [P, 2, D], F32)) for m in range(2)]
        ps_T = [ctx.enter_context(nc.psum_tensor(f"ro_psT{m}", [P, TILE], F32)) for m in range(KT)]
        ps_r = ctx.enter_context(nc.psum_tensor("ro_psr", [P, BLOCKS, E], F32))

        consts = sem("consts_landed")
        o_landed = sem("o_landed")
        x_landed = [sem(f"x_landed{k}") for k in range(2)]
        rec_ready = sem("rec_ready")
        att_ready = sem("att_ready")
        xb_ready = sem("xb_ready")
        y_psum = sem("y_psum")
        x1_ready = sem("x1_ready")
        chain_sem = sem("ln_chain")
        passed, passed_sp = sem("passed"), sem("passed_sp")
        var_ready, std_ready, x2_ready = sem("var_ready"), sem("std_ready"), sem("x2_ready")
        xT_psum = sem("xT_psum")
        xT_ready = sem("xT_ready")
        r_psum = sem("r_psum")
        r_ready = sem("r_ready")
        x1_stored = [sem(f"x1_stored{k}") for k in range(2)]
        xT_stored = [sem(f"xT_stored{k}") for k in range(2)]
        step_sem = sem("step")
        z_ready, exps = sem("z_ready"), sem("exps")
        w_stored = sem("w_stored")
        WEIGH_STEPS = E + 36
        z, den1, inh, zone, dist, w, fb, rest, top1, top2, order = (
            sb(name, [P, NB, E]) for name in "z den1 inh zone dist w fb rest top1 top2 order".split())
        total, none = sb("total", [P, NB]), sb("none", [P, NB])
        O_DMAS = 2 * H

        block = ctx.enter_context(nc.Block())

        @block.sync
        def _(sp):
            sp.dma_start(wo_sb[:], wo.rearrange("(k p) n -> p k n", p=P)).then_inc(consts, 16)
            sp.dma_start(bo_row[:], bo.rearrange("(a n) -> a n", a=1).to_broadcast([P, D])).then_inc(consts, 16)
            sp.dma_start(wr_sb[:], wr.rearrange("(k p) n -> p k n", p=P)).then_inc(consts, 16)
            sp.dma_start(temp[:], temperature.rearrange("(a n) -> a n", a=1).to_broadcast([P, 1])).then_inc(consts, 16)
            for k in range(2):
                sp.sem_inc(x1_stored[k], 16)
                sp.sem_inc(xT_stored[k], 16)
            with sp.Fori(0, B) as b:
                sp.wait_ge(att_ready, b * TILES_B + TILES_B)
                for h in range(H):
                    row = (h * HD) % P
                    for tile, skip in ((num, 0), (den, HD)):
                        sp.dma_start(tile[row:row + HD, h * HD // P, :],
                                     o_all[bass.ds(b * (H * VW) + (h * VW + skip), HD), :]).then_inc(o_landed, 16)
                for i in range(TILES_B):
                    k = i % 2
                    first = bass.ds(b * S + i * TILE, TILE)
                    sp.wait_ge(x1_ready, b * (2 * TILES_B) + (2 * i + 6))
                    sp.dma_start(x1_all[first, :].rearrange("(j p) d -> p j d", p=P), x1[k][:]).then_inc(x1_stored[k], 16)
                    wait_apart(sp, xT_ready, b * (KT * TILES_B) + KT * (i + 1), passed_sp)
                    sp.dma_start(x2T_all[:, first].rearrange("(m p) n -> p m n", p=P), x2T[k][:]).then_inc(xT_stored[k], 16)
            for k in range(2):
                sp.wait_ge(x1_stored[k], 16 * (TILES // 2 + 1))
                sp.wait_ge(xT_stored[k], 16 * (TILES // 2 + 1))

        @block.gpsimd
        def _(pool):
            pool.wait_ge(consts, 16 * 4)
            with pool.Fori(0, B) as b:
                for i in range(TILES_B):
                    k = i % 2
                    pool.wait_ge(x1_ready, b * (2 * TILES_B) + (2 * i + 2))
                    pool.dma_start(x_t[k][:], x_in[bass.ds(b * S + i * TILE, TILE), :].rearrange(
                        "(j p) d -> p j d", p=P)).then_inc(x_landed[k], 16)
                    pool.wait_ge(x_landed[k], b * 32 + 16 * (i // 2 + 1))
                    pool.tensor_tensor(xb[k][:], x_t[k][:], bo_row[:].unsqueeze(1).to_broadcast([P, BLOCKS, D]),
                                       ALU.add).then_inc(xb_ready, 1)
            pool.wait_ge(step_sem, WEIGH_STEPS)
            pool.dma_start(w_all.rearrange("(n p) e -> p n e", p=P), w[:]).then_inc(w_stored, 16)
            pool.wait_ge(w_stored, 16)

        @block.scalar
        def _(act):
            with act.Fori(0, B) as b:
                for i in range(TILES_B):
                    k = i % 2
                    t = b * TILES_B + i
                    act.wait_ge(var_ready, t + 1)
                    act.activation(small[:, 1, :], small[:, 0, :], ACT.Sqrt).then_inc(std_ready, 1)
                    act.wait_ge(xT_stored[k], b * 32 + 16 * (i // 2 + 1))
                    for m in range(KT):
                        act.wait_ge(xT_psum, t * KT + m + 1)
                        act.activation(x2T[k][:, m], ps_T[m][:], ACT.Identity).then_inc(xT_ready, 1)
            act.wait_ge(z_ready, 1)
            act.activation(z[:], z[:], ACT.Exp, scale=-1.0).then_inc(exps, 1)
            act.wait_ge(z_ready, 2)
            act.activation(w[:], dist[:], ACT.Exp, scale=-1.0 / 0.1).then_inc(exps, 1)
            act.activation(fb[:], dist[:], ACT.Exp, scale=-1.0 / 0.3).then_inc(exps, 1)

        @block.tensor
        def _(pe):
            pe.wait_ge(consts, 16 * 4)
            with pe.Fori(0, B) as b:
                for i in range(TILES_B):
                    k = i % 2
                    t = b * TILES_B + i
                    pe.wait_ge(att_ready, t + TILES_B + 1)
                    for m in range(2):
                        pe.wait_ge(x1_ready, t * 2 + m + 3)
                        for j in range(2):
                            for c in range(KT):
                                first = i * TILE + (2 * m + j) * P
                                ins = pe.matmul(ps_y[m][:, j], att[:, c, first:first + P], wo_sb[:, c],
                                                start=c == 0, stop=c == KT - 1)
                        ins.then_inc(y_psum, 1)
                    pe.wait_ge(x2_ready, t * BLOCKS + BLOCKS)
                    for m in range(KT):
                        for j in range(BLOCKS):
                            ins = pe.transpose(ps_T[m][:, j * P:(j + 1) * P], x2[k][:, j, m * P:(m + 1) * P], ident[:])
                        ins.then_inc(xT_psum, 1)
                    pe.wait_ge(xT_ready, t * KT + KT)
                    pe.wait_ge(r_ready, t + 1)
                    for j in range(BLOCKS):
                        for c in range(KT):
                            ins = pe.matmul(ps_r[:, j], x2T[k][:, c, j * P:(j + 1) * P], wr_sb[:, c],
                                            start=c == 0, stop=c == KT - 1)
                    ins.then_inc(r_psum, 1)

        @block.vector
        def _(dve):
            chain = Tally(chain_sem, LN_CHAIN)
            dve.sem_inc(att_ready, TILES_B)
            dve.sem_inc(x1_ready, 4)
            dve.sem_inc(r_ready, 1)
            with dve.Fori(0, B) as b:
                dve.wait_ge(o_landed, b * (16 * O_DMAS) + 16 * O_DMAS)
                for i in range(TILES_B):
                    k = i % 2
                    t = b * TILES_B + i
                    cols = slice(i * TILE, (i + 1) * TILE)
                    dve.reciprocal(den[:, :, cols], den[:, :, cols]).then_inc(rec_ready, 1)
                    dve.wait_ge(rec_ready, t + 1)
                    dve.tensor_tensor(att[:, :, cols], num[:, :, cols], den[:, :, cols], ALU.mult).then_inc(att_ready, 1)
                for i in range(TILES_B):
                    k = i % 2
                    t = b * TILES_B + i
                    dve.wait_ge(xb_ready, t + 1)
                    dve.wait_ge(x1_stored[k], b * 32 + 16 * (i // 2 + 1))
                    for m in range(2):
                        dve.wait_ge(y_psum, t * 2 + m + 1)
                        dve.tensor_tensor(x1[k][:, 2 * m:2 * m + 2], ps_y[m][:], xb[k][:, 2 * m:2 * m + 2],
                                          ALU.add).then_inc(x1_ready, 1)
                    dve.wait_ge(x1_ready, t * 2 + 6)
                    chain.start()
                    layer_norm(dve, chain, t, passed, x1[k], stats, moments, small, x2[k], var_ready, std_ready, x2_ready)
                    chain.end()
                    dve.wait_ge(r_psum, t + 1)
                    dve.tensor_copy(logits[:, bass.ds(t * BLOCKS, BLOCKS), :], ps_r[:]).then_inc(r_ready, 1)


            step = Tally(step_sem, WEIGH_STEPS)

            def do(instruction):
                step.up(instruction)
                step.wait(dve, 0)

            def over(column):
                return column.unsqueeze(2).to_broadcast([P, NB, E])

            tt, ts = dve.tensor_tensor, dve.tensor_scalar
            dve.wait_ge(r_ready, TILES + 1)
            for e in range(E):
                do(dve.memset(order[:, :, e], float(E - e)))
            do(dve.reciprocal(temp_r[:], temp[:]))
            ts(z[:], logits[:], temp_r[:, 0:1], None, ALU.mult).then_inc(z_ready, 1)
            dve.wait_ge(exps, 1)
            do(ts(den1[:], z[:], 1.0, None, ALU.add))
            do(dve.reciprocal(inh[:], den1[:]))
            do(ts(zone[:], inh[:], LOWER, None, ALU.is_ge))
            do(dve.scalar_tensor_tensor(out=zone[:], in0=inh[:], scalar=UPPER, in1=zone[:], op0=ALU.is_le, op1=ALU.mult))
            do(ts(inh[:], inh[:], CENTER, None, ALU.subtract))
            dve.scalar_tensor_tensor(out=dist[:], in0=inh[:], scalar=-1.0, in1=inh[:], op0=ALU.mult, op1=ALU.max).then_inc(z_ready, 1)
            dve.wait_ge(exps, 3)
            do(tt(w[:], w[:], zone[:], ALU.mult))
            do(dve.tensor_reduce(total[:], w[:], AX_X, ALU.add))
            do(ts(none[:], total[:], 1e-8, None, ALU.is_lt))
            do(dve.tensor_copy(rest[:], fb[:]))
            for mask in (top1, top2):
                do(dve.tensor_reduce(total[:], rest[:], AX_X, ALU.max))
                do(tt(mask[:], rest[:], over(total[:]), ALU.is_equal))
                do(tt(mask[:], mask[:], order[:], ALU.mult))
                do(dve.tensor_reduce(total[:], mask[:], AX_X, ALU.max))
                do(tt(mask[:], mask[:], over(total[:]), ALU.is_equal))
                do(dve.scalar_tensor_tensor(out=rest[:], in0=mask[:], scalar=-10.0, in1=rest[:], op0=ALU.mult, op1=ALU.add))
            do(tt(top1[:], top1[:], top2[:], ALU.add))
            do(tt(fb[:], fb[:], top1[:], ALU.mult))

            def normalise(x):
                do(dve.tensor_reduce(total[:], x[:], AX_X, ALU.add))
                do(ts(total[:], total[:], 1e-8, None, ALU.max))
                do(dve.reciprocal(total[:], total[:]))
                do(tt(x[:], x[:], over(total[:]), ALU.mult))

            normalise(fb)
            do(tt(fb[:], fb[:], over(none[:]), ALU.mult))
            do(ts(none[:], none[:], -1.0, 1.0, ALU.mult, ALU.add))
            do(tt(w[:], w[:], over(none[:]), ALU.mult))
            do(tt(w[:], w[:], fb[:], ALU.add))
            normalise(w)
            step.end()


SLICES = E * I // P
PASSES = ((0, 0), (0, 1), (1, 0))


def experts(nc, x2T_all, w_all, x1_all, wg, wu, wd, out):
    with ExitStack() as ctx:
        def sb(name, shape, dt=F32):
            return ctx.enter_context(nc.sbuf_tensor("ex_" + name, shape, dt))

        def sem(name):
            return ctx.enter_context(nc.semaphore("ex_" + name))

        wg_sb = [sb(f"wg{n}", [P, KT, E * I], F32R) for n in range(2)]
        wu_sb = [sb(f"wu{n}", [P, KT, E * I], F32R) for n in range(2)]
        wd_sb = [sb(f"wd{n}", [P, SLICES, D], F32R) for n in range(2)]
        x2_f = [sb(f"x2f{k}", [P, KT, TILE]) for k in range(2)]
        x2_s = [[sb(f"x2s{k}{n}", [P, KT, TILE], F32R) for n in range(2)] for k in range(2)]
        w_row = [sb(f"wrow{k}", [P, TILE, E]) for k in range(2)]
        stage = [w_row[k][:].rearrange("p n e -> p (n e)")[:, 0:E * I] for k in range(2)]
        silu = [sb(f"silu{k}", [P, TILE]) for k in range(2)]
        up_w = sb("up_w", [P, TILE])
        h_f = sb("h_f", [P, TILE])
        h_s = [[sb(f"h{k}{n}", [P, TILE], F32R) for n in range(2)] for k in range(2)]
        x1_t = [sb(f"x1{k}", [P, BLOCKS, D]) for k in range(2)]
        out_t = [sb(f"out{k}", [P, BLOCKS, D]) for k in range(2)]
        ps_g = [ctx.enter_context(nc.psum_tensor(f"ex_psg{m}", [P, TILE], F32)) for m in range(2)]
        ps_u = [ctx.enter_context(nc.psum_tensor(f"ex_psu{m}", [P, TILE], F32)) for m in range(2)]
        ps_d = [ctx.enter_context(nc.psum_tensor(f"ex_psd{m}", [P, TILE], F32)) for m in range(BLOCKS)]

        staged = [sem(f"staged{k}") for k in range(2)]
        high_ready = sem("high_ready")
        low_ready = sem("low_ready")
        x2_landed = [sem(f"x2_landed{k}") for k in range(2)]
        w_landed = [sem(f"w_landed{k}") for k in range(2)]
        x1_landed = [sem(f"x1_landed{k}") for k in range(2)]
        passed = sem("passed")
        x2_split = sem("x2_split")
        gu_psum = sem("gu_psum")
        silu_ready = sem("silu_ready")
        up_ready = sem("up_ready")
        h_ready = sem("h_ready")
        h_high = sem("h_high")
        h_low = sem("h_low")
        down_done = sem("down_done")
        y_ready = sem("y_ready")
        out_stored = [sem(f"out_stored{k}") for k in range(2)]

        chunks = []
        for w, tiles in ((wg, wg_sb), (wu, wu_sb)):
            for c in range(KT):
                chunks.append((w[:, c * P:(c + 1) * P, :].rearrange("e p i -> p e i"), E, [x[:, c] for x in tiles]))
        for c in range(2):
            half = SLICES // 2
            src = wd.rearrange("e (s p) d -> p (e s) d", p=P)[:, c * half:(c + 1) * half]
            chunks.append((src, half, [x[:, c * half:(c + 1) * half].rearrange("p s d -> p (s d)") for x in wd_sb]))

        block = ctx.enter_context(nc.Block())

        @block.sync
        def _(sp):
            def load(t, k):
                first = bass.ds(t * TILE, TILE)
                sp.dma_start(x2_f[k][:], x2T_all[:, first].rearrange("(m p) n -> p m n", p=P)).then_inc(x2_landed[k], 16)
                sp.dma_start(x1_t[k][:], x1_all[first, :].rearrange("(j p) d -> p j d", p=P)).then_inc(x1_landed[k], 16)

            def load_w(t, k):
                sp.dma_start(w_row[k][:].rearrange("p n e -> p (n e)"),
                             w_all[bass.ds(t * TILE, TILE), :].rearrange("(a n) e -> a (n e)", a=1).to_broadcast([P, TILE * E])).then_inc(w_landed[k], 16)

            def store(t, k):
                sp.wait_ge(y_ready, t * BLOCKS + 2 * BLOCKS)
                sp.dma_start(out[bass.ds(t * TILE, TILE), :].rearrange("(j p) d -> p j d", p=P), out_t[k][:]).then_inc(out_stored[k], 16)

            for n, (src, parts, _) in enumerate(chunks):
                if n >= 2:
                    sp.wait_ge(low_ready, n - 1)
                sp.dma_start(stage[n % 2].rearrange("p (a b) -> p a b", a=parts), src).then_inc(staged[n % 2], 16)
            for k in range(2):
                load(k, k)
                sp.wait_ge(low_ready, len(chunks) - 1 + k)
                load_w(k, k)
            with sp.Fori(0, TILES // 2 - 1) as it:
                for k in range(2):
                    store(it * 2 + k, k)
                    load(it * 2 + (k + 2), k)
                    load_w(it * 2 + (k + 2), k)
            for k in range(2):
                store(TILES - 2 + k, k)
            for k in range(2):
                sp.wait_ge(out_stored[k], 16 * (TILES // 2 + 1))

        @block.gpsimd
        def _(pool):
            with pool.Fori(0, TILES // 2) as it:
                for k in range(2):
                    t = it * 2 + k
                    pool.wait_ge(x2_landed[k], it * 16 + 16)
                    wait_apart(pool, gu_psum, t * SLICES + SLICES, passed)
                    pool.tensor_copy(x2_s[k][0][:], x2_f[k][:]).then_inc(x2_split, 1)
                    pool.wait_ge(x2_split, t * 2 + 1)
                    pool.tensor_tensor(x2_s[k][1][:], x2_f[k][:], x2_s[k][0][:].bitcast(F32), ALU.subtract).then_inc(x2_split, 1)

        @block.scalar
        def _(act):
            with act.Fori(0, TILES) as t:
                for s in range(SLICES):
                    act.wait_ge(gu_psum, t * SLICES + (2 * SLICES + s + 1))
                    act.activation(silu[s % 2][:], ps_g[s % 2][:], ACT.Silu).then_inc(silu_ready, 1)

        @block.vector
        def _(dve):
            dve.sem_inc(y_ready, BLOCKS)
            for k in range(2):
                dve.sem_inc(out_stored[k], 16)
            for n, (_, _, halves) in enumerate(chunks):
                dve.wait_ge(staged[n % 2], 16 * (n // 2 + 1))
                dve.tensor_copy(halves[0], stage[n % 2]).then_inc(high_ready, 1)
                dve.wait_ge(high_ready, n + 1)
                dve.tensor_tensor(halves[1], stage[n % 2], halves[0].bitcast(F32), ALU.subtract).then_inc(low_ready, 1)
            with dve.Fori(0, TILES // 2) as it:
                for k in range(2):
                    t = it * 2 + k
                    dve.wait_ge(w_landed[k], it * 16 + 16)
                    for s in range(SLICES):
                        dve.wait_ge(gu_psum, t * SLICES + (2 * SLICES + s + 1))
                        dve.tensor_tensor(up_w[:], ps_u[s % 2][:], w_row[k][:, :, s * P // I], ALU.mult).then_inc(up_ready, 1)
                        dve.wait_ge(up_ready, t * SLICES + (s + 1))
                        dve.wait_ge(silu_ready, t * SLICES + (s + 1))
                        dve.tensor_tensor(h_f[:], up_w[:], silu[s % 2][:], ALU.mult).then_inc(h_ready, 1)
                        dve.wait_ge(h_ready, t * SLICES + (s + 1))
                        dve.wait_ge(down_done, t * SLICES + (s + 1))
                        dve.tensor_copy(h_s[s % 2][0][:], h_f[:]).then_inc(h_high, 1)
                        dve.wait_ge(h_high, t * SLICES + (s + 1))
                        dve.tensor_tensor(h_s[s % 2][1][:], h_f[:], h_s[s % 2][0][:].bitcast(F32), ALU.subtract).then_inc(h_low, 1)
                    dve.wait_ge(down_done, t * SLICES + (SLICES + 2))
                    dve.wait_ge(x1_landed[k], it * 16 + 16)
                    dve.wait_ge(out_stored[k], it * 16 + 16)
                    for j in range(BLOCKS):
                        dve.tensor_tensor(out_t[k][:, j], ps_d[j][:, 0:D], x1_t[k][:, j], ALU.add).then_inc(y_ready, 1)

        @block.tensor
        def _(pe):
            def gate_up(t, k, s, free=True):
                if s == 0:
                    pe.wait_ge(x2_split, t * 2 + 2)
                if free:
                    pe.wait_ge(h_ready, t * SLICES + (s - 1))
                for ps, w in ((ps_g[s % 2], wg_sb), (ps_u[s % 2], wu_sb)):
                    for c in range(KT):
                        for n, (wh, xh) in enumerate(PASSES):
                            ins = pe.matmul(ps[:], w[wh][:, c, s * P:(s + 1) * P], x2_s[k][xh][:, c],
                                            start=c == 0 and n == 0, stop=c == KT - 1 and n == len(PASSES) - 1)
                ins.then_inc(gu_psum, 1)

            def down(t, s):
                pe.wait_ge(h_low, t * SLICES + (s + 1))
                for j in range(BLOCKS):
                    if s == 0:
                        pe.wait_ge(y_ready, t * BLOCKS + BLOCKS)
                    for n, (wh, hh) in enumerate(PASSES):
                        ins = pe.matmul(ps_d[j][:, 0:D], h_s[s % 2][hh][:, j * P:(j + 1) * P], wd_sb[wh][:, s],
                                        start=s == 0 and n == 0, stop=s == SLICES - 1 and n == len(PASSES) - 1)
                ins.then_inc(down_done, 1)

            def tile(t, k, after=True):
                for s in range(SLICES):
                    if s + 2 < SLICES:
                        gate_up(t, k, s + 2)
                    elif after:
                        gate_up(t + 1, 1 - k, s + 2 - SLICES)
                    down(t, s)

            pe.sem_inc(gu_psum, 2 * SLICES)
            pe.sem_inc(down_done, 2)
            pe.wait_ge(low_ready, len(chunks))
            for s in range(2):
                gate_up(0, 0, s, free=False)
            with pe.Fori(0, TILES // 2 - 1) as it:
                for k in range(2):
                    tile(it * 2 + k, k)
            tile(TILES - 2, 0)
            tile(TILES - 1, 1, after=False)


def build(nc, x, wq, bq, wk, bk, wv, bv, wo, bo, wg, wu, wd, wr, temperature, out):
    def scratch(name, shape):
        return nc.dram_tensor(name, shape, F32, kind="Internal").ap()

    q_hi, q_lo, k_hi, k_lo = (scratch(name, (B * D, S)) for name in ("q_hi", "q_lo", "k_hi", "k_lo"))
    v_all = scratch("v_all", (B * GROUPS_B, S, G * VW))
    o_all = scratch("o_all", (B * H * VW, S))
    m_all = scratch("m_all", (GROUPS * P, P))
    x1_all = scratch("x1_all", (B * S, D))
    x2T_all = scratch("x2T_all", (D, B * S))
    w_all = scratch("w_all", (B * S, E))
    x_in, y_out = x.rearrange("b s d -> (b s) d"), out.rearrange("b s d -> (b s) d")
    with ExitStack() as ctx:
        ident = ctx.enter_context(nc.sbuf_tensor("ident", [P, P], F32))
        made = ctx.enter_context(nc.semaphore("ident_made"))
        with nc.Block() as block:
            @block.gpsimd
            def _(pool):
                pool.memset(ident[:], 0.0).then_inc(made, 1)
                pool.wait_ge(made, 1)
                pool.affine_select(out=ident[:], in_=ident[:], compare_op=ALU.not_equal, fill=1.0, base=0,
                                   pattern=[[-1, P]], channel_multiplier=1).then_inc(made, 1)
                pool.wait_ge(made, 2)
        project(nc, ident, x_in, wq, bq, wk, bk, wv, bv, q_hi, q_lo, k_hi, k_lo, v_all)
        attend(nc, ident, q_hi, q_lo, k_hi, k_lo, v_all, m_all, o_all)
        route(nc, ident, x_in, o_all, wo, bo, wr, temperature, x1_all, x2T_all, w_all)
        experts(nc, x2T_all, w_all, x1_all, wg, wu, wd, y_out)


_INS = ["L0_attn_x", "L0_attn_wq", "L0_attn_bq", "L0_attn_wk", "L0_attn_bk", "L0_attn_wv", "L0_attn_bv",
        "L0_attn_wo", "L0_attn_bo", "L0_ffn_Wg", "L0_ffn_Wu", "L0_ffn_Wd", "L0_ffn_Wr", "L0_ffn_temperature"]


def kernel(**inputs):
    import numpy as _np
    import concourse.bacc as _bacc
    from concourse import mybir as _mybir
    from concourse.bass_utils import run_bass_kernel_spmd as _run

    nc = _bacc.Bacc("TRN2", target_bir_lowering=False, num_devices=1)
    arrays, args = {}, []
    for name in _INS:
        a = _np.ascontiguousarray(inputs[name])
        arrays[f"in_{name}_dram"] = a
        args.append(nc.dram_tensor(f"in_{name}_dram", a.shape, _mybir.dt.from_np(a.dtype), kind="ExternalInput").ap())
    args.append(nc.dram_tensor("out_0_dram", (B, S, D), _mybir.dt.float32, kind="ExternalOutput").ap())
    build(nc, *args)
    r = _run(nc, [arrays], core_ids=[0])
    return r.results[0]["out_0_dram"]
```

```python
import math
from contextlib import ExitStack

import concourse.bass as bass
from concourse import mybir

F32 = mybir.dt.float32
F32R = mybir.dt.float32r
BF16 = mybir.dt.bfloat16
ALU = mybir.AluOpType
ACT = mybir.ActivationFunctionType
AX_X = mybir.AxisListType.X

P = 128
B, S, D = 4, 2048, 256
H, HD = 16, 16
E, I = 8, 256
KT = D // P
TILE = 512
BLOCKS = TILE // P
TILES_B = S // TILE
TILES = B * TILES_B
G = 4
GROUPS_B = H // G
GROUPS = B * GROUPS_B
VW = 2 * HD
EPS = 1e-5
LOW = -3.0e38


def wait_apart(engine, sem, value, passed):
    engine.wait_ge(sem, value)
    engine.sem_inc(passed, 1)


class Tally:

    def __init__(self, sem, per_tile):
        self.sem, self.per_tile, self.count = sem, per_tile, 0

    def start(self):
        self.count = 0

    def up(self, instruction):
        instruction.then_inc(self.sem, 1)
        self.count += 1

    def wait(self, engine, tile):
        engine.wait_ge(self.sem, tile * self.per_tile + self.count)

    def end(self):
        assert self.count == self.per_tile, (self.count, self.per_tile)


def layer_norm(dve, chain, tile, passed, x, stats, moments, small, xn, var_ready, std_ready, xn_ready):
    for j in range(BLOCKS):
        chain.up(dve.bn_stats(stats[:, j, :], x[:, j, :]))
    wait_apart(dve, chain.sem, tile * chain.per_tile + chain.count, passed)
    for j in range(BLOCKS):
        chain.up(dve.bn_aggr(moments[:, j, :], stats[:, j, :]))
    chain.wait(dve, tile)
    var, std, rec, tmp = (small[:, n, :] for n in range(4))
    dve.tensor_scalar(var, moments[:, :, 1], EPS, None, ALU.add).then_inc(var_ready, 1)
    dve.wait_ge(var_ready, tile + 1)
    dve.wait_ge(std_ready, tile + 1)
    chain.up(dve.reciprocal(rec, std))
    chain.wait(dve, tile)
    chain.up(dve.tensor_tensor(tmp, var, rec, ALU.mult))
    chain.wait(dve, tile)
    chain.up(dve.tensor_tensor(std, std, tmp, ALU.add))
    chain.wait(dve, tile)
    chain.up(dve.tensor_scalar(tmp, std, 0.5, None, ALU.mult))
    chain.wait(dve, tile)
    chain.up(dve.reciprocal(rec, tmp))
    chain.wait(dve, tile)
    for j in range(BLOCKS):
        dve.tensor_scalar(xn[:, j, :], x[:, j, :], moments[:, j, 0:1], rec[:, j:j + 1],
                          ALU.subtract, ALU.mult).then_inc(xn_ready, 1)


LN_CHAIN = 4 + 4 + 5


def project(nc, ident, x_in, wq, bq, wk, bk, wv, bv, q_hi, q_lo, k_hi, k_lo, v_all):
    with ExitStack() as ctx:
        def sb(name, shape, dt=F32):
            return ctx.enter_context(nc.sbuf_tensor("pr_" + name, shape, dt))

        def sem(name):
            return ctx.enter_context(nc.semaphore("pr_" + name))

        w_sb = sb("w", [P, 3, KT, D])
        bias_col = sb("bias_col", [P, 2, KT])
        bv_row = sb("bv_row", [P, 2, D])
        x_t = [sb(f"x{k}", [P, BLOCKS, D]) for k in range(2)]
        stats = sb("stats", [P, BLOCKS, 6])
        moments = sb("moments", [P, BLOCKS, 2])
        small = sb("small", [P, 4, BLOCKS])
        xn = [sb(f"xn{k}", [P, BLOCKS, D]) for k in range(2)]
        xnT = [sb(f"xnT{k}", [P, KT, TILE]) for k in range(2)]
        qk_f = [sb(f"qk_f{k}", [P, 2 * KT, TILE]) for k in range(2)]
        qk_h = [sb(f"qk_h{k}", [P, 2 * KT, TILE], F32R) for k in range(2)]
        qk_l = [sb(f"qk_l{k}", [P, 2 * KT, TILE], F32R) for k in range(2)]
        v_t = [sb(f"v{k}", [P, BLOCKS, H, VW]) for k in range(2)]
        ps_T = [ctx.enter_context(nc.psum_tensor(f"pr_psT{m}", [P, TILE], F32)) for m in range(KT)]
        ps_qk = [ctx.enter_context(nc.psum_tensor(f"pr_psqk{m}", [P, TILE], F32)) for m in range(4)]
        ps_v = [ctx.enter_context(nc.psum_tensor(f"pr_psv{m}", [P, 2, D], F32)) for m in range(2)]

        consts = sem("consts_landed")
        ones = sem("v_ones")
        x_landed = [sem(f"x_landed{k}") for k in range(2)]
        chain_sem = sem("ln_chain")
        passed = sem("passed")
        var_ready, std_ready, xn_ready = sem("var_ready"), sem("std_ready"), sem("xn_ready")
        xT_psum = sem("xT_psum")
        xT_ready = sem("xT_ready")
        qk_psum = sem("qk_psum")
        v_psum = sem("v_psum")
        qk_full = sem("qk_full")
        hi_ready = sem("hi_ready")
        lo_ready = sem("lo_ready")
        v_ready = sem("v_ready")
        stored = [sem(f"stored{k}") for k in range(2)]

        STORES = 4 + BLOCKS
        block = ctx.enter_context(nc.Block())

        @block.sync
        def _(sp):
            for n, w in enumerate((wq, wk, wv)):
                sp.dma_start(w_sb[:, n], w.rearrange("(k p) n -> p k n", p=P)).then_inc(consts, 16)
            for n, bias in enumerate((bq, bk)):
                sp.dma_start(bias_col[:, n], bias.rearrange("(k p) -> p k", p=P),
                             allow_slow_non_contiguous=True).then_inc(consts, 16)
            for n in range(2):
                sp.dma_start(bv_row[:, n], bv.rearrange("(a n) -> a n", a=1).to_broadcast([P, D])).then_inc(consts, 16)
            for k in range(2):
                sp.sem_inc(stored[k], 16 * STORES)
                sp.dma_start(x_t[k][:], x_in[k * TILE:(k + 1) * TILE, :].rearrange(
                    "(j p) d -> p j d", p=P)).then_inc(x_landed[k], 16)

            def store(b, t, j, k):
                sp.wait_ge(lo_ready, t * 4 + 4)
                sp.wait_ge(v_ready, t * 2 + 4)
                rows, cols = bass.ds(b * D, D), bass.ds(j * (2 * TILE) + k * TILE, TILE)
                for dram, tile, m in ((q_hi, qk_h, 0), (q_lo, qk_l, 0), (k_hi, qk_h, 2), (k_lo, qk_l, 2)):
                    sp.dma_start(dram[rows, cols].rearrange("(m p) n -> p m n", p=P),
                                 tile[k][:, m:m + 2].bitcast(F32)).then_inc(stored[k], 16)
                for i in range(BLOCKS):
                    sp.dma_start(
                        v_all[bass.ds(b * GROUPS_B, GROUPS_B),
                              bass.ds(j * (2 * TILE) + (k * TILE + i * P), P), :].rearrange("g p n -> p g n"),
                        v_t[k][:, i].rearrange("p (g h) n -> p g (h n)", h=G)).then_inc(stored[k], 16)

            def pair(b, j, load):
                for k in range(2):
                    t = b * TILES_B + j * 2 + k
                    if load:
                        sp.wait_ge(xn_ready, t * BLOCKS + BLOCKS)
                        sp.dma_start(x_t[k][:], x_in[bass.ds(b * S + j * (2 * TILE) + (k + 2) * TILE, TILE), :].rearrange(
                            "(j p) d -> p j d", p=P)).then_inc(x_landed[k], 16)
                    store(b, t, j, k)

            with sp.Fori(0, B - 1) as b:
                with sp.Fori(0, TILES_B // 2) as j:
                    pair(b, j, True)
            for j in range(TILES_B // 2):
                pair(B - 1, j, j < TILES_B // 2 - 1)
            for k in range(2):
                sp.wait_ge(stored[k], 16 * STORES * (TILES // 2 + 1))

        @block.gpsimd
        def _(pool):
            for k in range(2):
                pool.memset(v_t[k][:], 1.0).then_inc(ones, 1)
            with pool.Fori(0, B) as b:
                with pool.Fori(0, TILES_B // 2) as j:
                    for k in range(2):
                        t = b * TILES_B + j * 2 + k
                        n = b * (TILES_B // 2) + j
                        pool.wait_ge(stored[k], n * (16 * STORES) + 16 * STORES)
                        for m in range(4):
                            pool.wait_ge(hi_ready, t * 4 + m + 1)
                            pool.tensor_tensor(qk_l[k][:, m], qk_f[k][:, m], qk_h[k][:, m].bitcast(F32),
                                               ALU.subtract).then_inc(lo_ready, 1)

        @block.scalar
        def _(act):
            def root(t):
                act.wait_ge(var_ready, t + 1)
                act.activation(small[:, 1, :], small[:, 0, :], ACT.Sqrt).then_inc(std_ready, 1)

            def transposed(t, k):
                for m in range(KT):
                    act.wait_ge(xT_psum, t * KT + m + 1)
                    act.activation(xnT[k][:, m], ps_T[m][:], ACT.Identity).then_inc(xT_ready, 1)

            def with_bias(t, k, nth, after):
                act.wait_ge(stored[k], nth * (16 * STORES) + 16 * STORES)
                for m in range(4):
                    act.wait_ge(qk_psum, t * 4 + m + 1)
                    act.activation(qk_f[k][:, m], ps_qk[m][:], ACT.Identity,
                                   bias=bias_col[:, m // 2, m % 2:m % 2 + 1]).then_inc(qk_full, 1)
                    if m == 1 and after:
                        root(t + 1)
                if after:
                    transposed(t + 1, 1 - k)

            act.sem_inc(qk_full, 4)
            act.wait_ge(consts, 16 * 7)
            root(0)
            transposed(0, 0)
            with act.Fori(0, TILES // 2 - 1) as it:
                for k in range(2):
                    with_bias(it * 2 + k, k, it, True)
            for k in range(2):
                with_bias(TILES - 2 + k, k, TILES // 2 - 1, k == 0)

        @block.vector
        def _(dve):
            chain = Tally(chain_sem, LN_CHAIN)

            def normalise(t, k, nth):
                dve.wait_ge(x_landed[k], nth * 16 + 16)
                chain.start()
                layer_norm(dve, chain, t, passed, x_t[k], stats, moments, small, xn[k],
                           var_ready, std_ready, xn_ready)
                chain.end()

            def tile(t, k, nth, after):
                if after:
                    normalise(t + 1, 1 - k, nth + k)
                dve.wait_ge(stored[k], nth * (16 * STORES) + 16 * STORES)
                for m in range(4):
                    dve.wait_ge(qk_full, t * 4 + m + 5)
                    dve.tensor_copy(qk_h[k][:, m], qk_f[k][:, m]).then_inc(hi_ready, 1)
                for m in range(2):
                    dve.wait_ge(v_psum, t * 2 + m + 1)
                    dve.tensor_tensor(
                        v_t[k][:, 2 * m:2 * m + 2, :, 0:HD].rearrange("p j h c -> p (j h) c"),
                        ps_v[m][:].rearrange("p j (h c) -> p (j h) c", c=HD),
                        bv_row[:].rearrange("p j (h c) -> p (j h) c", c=HD), ALU.add).then_inc(v_ready, 1)

            dve.sem_inc(v_ready, 2)
            dve.wait_ge(consts, 16 * 7)
            dve.wait_ge(ones, 2)
            normalise(0, 0, 0)
            with dve.Fori(0, TILES // 2 - 1) as it:
                for k in range(2):
                    tile(it * 2 + k, k, it, True)
            for k in range(2):
                tile(TILES - 2 + k, k, TILES // 2 - 1, k == 0)

        @block.tensor
        def _(pe):
            def transpose(t, k):
                pe.wait_ge(xn_ready, t * BLOCKS + BLOCKS)
                for m in range(KT):
                    for j in range(BLOCKS):
                        ins = pe.transpose(ps_T[m][:, j * P:(j + 1) * P], xn[k][:, j, m * P:(m + 1) * P], ident[:])
                    ins.then_inc(xT_psum, 1)

            def tile(t, k, after):
                pe.wait_ge(xT_ready, t * KT + KT)
                for m in range(4):
                    pe.wait_ge(qk_full, t * 4 + m + 1)
                    for c in range(KT):
                        ins = pe.matmul(ps_qk[m][:], w_sb[:, m // 2, c, (m % 2) * P:(m % 2 + 1) * P],
                                        xnT[k][:, c], start=(c == 0), stop=(c == KT - 1))
                    ins.then_inc(qk_psum, 1)
                if after:
                    transpose(t + 1, 1 - k)
                for m in range(2):
                    pe.wait_ge(v_ready, t * 2 + m + 1)
                    for j in range(2):
                        for c in range(KT):
                            ins = pe.matmul(ps_v[m][:, j], xnT[k][:, c, (2 * m + j) * P:(2 * m + j + 1) * P],
                                            w_sb[:, 2, c], start=(c == 0), stop=(c == KT - 1))
                    ins.then_inc(v_psum, 1)

            pe.wait_ge(consts, 16 * 7)
            transpose(0, 0)
            with pe.Fori(0, TILES // 2 - 1) as it:
                for k in range(2):
                    tile(it * 2 + k, k, True)
            tile(TILES - 2, 0, True)
            tile(TILES - 1, 1, False)


UNITS = [(j, kb, max(0, kb - BLOCKS * j) * P) for j in reversed(range(TILES_B)) for kb in range(BLOCKS * (j + 1))]
LAST = {max(u for u, x in enumerate(UNITS) if x[0] == j): j for j in range(TILES_B)}
NU = len(UNITS)
AHEAD = 2
RING = 4
QB = S // P
LATER = 4
BANKS = 3
KMAX = P - 2
KSCORE = P


def max_items():
    items = []
    for j in reversed(range(TILES_B)):
        for h in range(0, G, 2):
            for head in (h, h + 1):
                items.append(("chunk", j, j, [(head, 3, 0, 4 * P)]))
                items.append(("chunk", j, j, [(head, 2, 0, 3 * P), (head, 0, 3 * P, P)]))
            pair = [(h, 1, 0, 2 * P), (h + 1, 1, 2 * P, 2 * P)]
            items += [("chunk", j, j, [x]) for x in pair] if (j, h) == (0, 0) else [("chunk", j, j, pair)]
        for c in reversed(range(j)):
            items += [("chunk", j, c, [(h, i, 0, TILE)]) for i in range(BLOCKS) for h in range(G)]
    for j in range(TILES_B):
        last = max(y for y, x in enumerate(items) if x[0] == "chunk" and x[1] == j)
        items.insert(min(last + 1 + LATER, len(items)), ("rows", j))
    return items


ITEMS = max_items()
NI = len(ITEMS)
FIRST_ROWS = ITEMS.index(("rows", TILES_B - 1)) + 1
LAST_CHUNK = {max(y for y, x in enumerate(ITEMS) if x[0] == "chunk" and x[1] == j): j for j in range(TILES_B)}
assert NI % BANKS == 0
ITEMS_BY = 0.93


def item_plan():
    items = [(0, y) for y in range(FIRST_ROWS, NI)] + [(1, y) for y in range(FIRST_ROWS)]

    def vector_time(y):
        return 900 if ITEMS[y][0] == "rows" else TILE + 120

    pieces = [w for u in UNITS for w in (2 * (TILE - u[2]), 2 * (TILE - u[2]), 4 * (TILE - u[2]))]
    whole, plan, at, done, spent = sum(vector_time(y) for _, y in items), [], 0, 0, 0
    for w in pieces:
        at += w
        piece = []
        while done < len(items) and (spent <= whole * at / (ITEMS_BY * sum(pieces)) or at == sum(pieces)):
            piece.append(items[done])
            spent += vector_time(items[done][1])
            done += 1
        plan.append(piece)
    return plan


def attend(nc, ident, q_hi, q_lo, k_hi, k_lo, v_all, m_all, o_all):
    with ExitStack() as ctx:
        def sb(name, shape, dt=F32):
            return ctx.enter_context(nc.sbuf_tensor("at_" + name, shape, dt))

        def sem(name):
            return ctx.enter_context(nc.semaphore("at_" + name))

        q_st = [sb(f"q{k}", [KSCORE, G, S], F32R) for k in range(2)]
        k_st = [sb(f"k{k}", [KSCORE, G, S], F32R) for k in range(2)]
        v_st = [sb(f"v{k}", [P, QB, G * VW]) for k in range(2)]
        probs = [sb(f"probs{r}", [P, G, TILE]) for r in range(RING)]
        mask = sb("mask", [P, P], BF16)
        ident16 = sb("ident16", [P, P], BF16)
        part = sb("part", [P, TILES_B, G, BLOCKS, TILES_B])
        row_max = sb("row_max", [P, G, BLOCKS])
        max_h = sb("max_h", [P, G * BLOCKS], F32R)
        neg_max = sb("neg_max", [P, TILES_B, 2, G * BLOCKS])
        max_rows = sb("max_rows", [P, P], F32R)
        o_sb = [sb(f"o{k}", [P, TILE]) for k in range(2)]
        ps_s = [ctx.enter_context(nc.psum_tensor(f"at_pss{m}", [P, 2, TILE], F32)) for m in range(2)]
        ps_m = [ctx.enter_context(nc.psum_tensor(f"at_psm{m}", [P, TILE], F32)) for m in range(BANKS)]
        ps_o = ctx.enter_context(nc.psum_tensor("at_pso", [P, TILE], F32))

        mask_zero = sem("mask_zero")
        passed_dve, passed_pool, passed_sp = sem("passed_dve"), sem("passed_pool"), sem("passed_sp")
        init = sem("init")
        landed = [[sem(f"landed{k}{c}") for c in range(TILES_B)] for k in range(2)]
        v_landed = [sem(f"v_landed{k}") for k in range(2)]
        item_psum = sem("item_psum")
        item_done = sem("item_done")
        max_step = sem("max_step")
        rows_saved = sem("rows_saved")
        rows_landed = [sem(f"rows_landed{j}") for j in range(TILES_B)]
        score_psum = sem("score_psum")
        exp_ready = sem("exp_ready")
        masked = sem("masked")
        unit_done = sem("unit_done")
        o_ready = sem("o_ready")
        o_stored = [sem(f"o_stored{k}") for k in range(2)]

        block = ctx.enter_context(nc.Block())
        QUARTER = 8 * 16
        MAX_STEPS = 4

        def load_quarter(sp, n, k, c):
            cols = slice(c * TILE, (c + 1) * TILE)
            rows = bass.ds(n * (G * HD), G * HD)
            for stack, halves in ((q_st[k], (q_hi, q_hi, q_lo, q_lo)), (k_st[k], (k_hi, k_lo, k_hi, k_lo))):
                for slot, dram in enumerate(halves):
                    sp.dma_start(stack[slot * HD:(slot + 1) * HD, :, cols].bitcast(F32),
                                 dram[rows, cols].rearrange("(h r) n -> r h n", r=HD)).then_inc(landed[k][c], 16)

        def load_v(sp, n, k):
            for c in range(TILES_B):
                sp.dma_start(v_st[k][:, c * BLOCKS:(c + 1) * BLOCKS],
                             v_all[bass.ds(n, 1), c * TILE:(c + 1) * TILE, :].rearrange(
                                 "a (i p) n -> p (a i) n", p=P)).then_inc(v_landed[k], 16)

        @block.sync
        def _(sp):
            def store_maxima(n, k, j):
                nth = n * TILES_B + (TILES_B - 1 - j)
                done = n * NI + (ITEMS.index(("rows", j)) + 1)
                wait_apart(sp, item_done, done, passed_sp)
                rows = bass.ds(n * P + j * (P // TILES_B), P // TILES_B)
                sp.dma_start(m_all[rows, :], max_rows[j * (P // TILES_B):(j + 1) * (P // TILES_B)].bitcast(F32)).then_inc(rows_saved, 16)
                wait_apart(sp, rows_saved, nth * 16 + 16 * (TILES_B + 1), passed_sp)
                sp.dma_start(q_st[k][KMAX:KSCORE, :, j * TILE:(j + 1) * TILE].bitcast(F32),
                             m_all[rows, :].rearrange("(a h i) n -> a h (i n)", a=2, h=G)).then_inc(rows_landed[j], 16)

            def next_quarter(n, k, c):
                last = max(u for u, x in enumerate(UNITS) if x[0] == c)
                wait_apart(sp, score_psum, n * (2 * NU) + 2 * (last + 1), passed_sp)
                load_quarter(sp, n + 2, k, c)

            def store_output(n, j):
                wait_apart(sp, o_ready, n * TILES_B + (TILES_B - j + 1), passed_sp)
                sp.dma_start(o_all[bass.ds(n * P, P), j * TILE:(j + 1) * TILE], o_sb[j % 2][:]).then_inc(o_stored[j % 2], 16)

            def group(n, k, load=True, after=True):
                store_maxima(n, k, 2)
                if load:
                    next_quarter(n, k, 3)
                store_output(n, 3)
                store_maxima(n, k, 1)
                store_maxima(n, k, 0)
                if load:
                    next_quarter(n, k, 2)
                store_output(n, 2)
                if load:
                    next_quarter(n, k, 1)
                if after:
                    store_maxima(n + 1, 1 - k, 3)
                store_output(n, 1)
                if load:
                    next_quarter(n, k, 0)
                store_output(n, 0)
                if load:
                    load_v(sp, n + 2, k)

            sp.wait_ge(init, 8)
            for n in range(2):
                for c in reversed(range(TILES_B)):
                    load_quarter(sp, n, n, c)
                load_v(sp, n, n)
            store_maxima(0, 0, 3)
            with sp.Fori(0, GROUPS // 2 - 1) as it:
                for k in range(2):
                    group(it * 2 + k, k)
            group(GROUPS - 2, 0, load=False)
            group(GROUPS - 1, 1, load=False, after=False)
            for k in range(2):
                sp.wait_ge(o_stored[k], 16 * (2 * GROUPS + 1))

        @block.gpsimd
        def _(pool):
            pool.memset(mask[:], 0.0).then_inc(mask_zero, 1)
            pool.wait_ge(mask_zero, 1)
            pool.affine_select(out=mask[:], in_=mask[:], compare_op=ALU.is_ge, fill=LOW,
                               base=0, pattern=[[-1, P]], channel_multiplier=1).then_inc(init, 1)
            with pool.Fori(0, GROUPS) as n:
                for u, (j, kb, first) in enumerate(UNITS):
                    if kb < BLOCKS * j:
                        continue
                    wait_apart(pool, exp_ready, n * (2 * NU) + 2 * (u + 1), passed_pool)
                    diagonal = probs[u % RING][:, :, first:first + P]
                    pool.affine_select(out=diagonal, in_=diagonal, compare_op=ALU.is_ge, fill=0.0, base=0,
                                       pattern=[[0, G], [1, P]], channel_multiplier=-1).then_inc(masked, 1)

        @block.scalar
        def _(act):
            def exponentials(n, u):
                _, _, first = UNITS[u]
                for half in range(2):
                    act.wait_ge(score_psum, n * (2 * NU) + 2 * u + half + 1)
                    act.activation(probs[u % RING][:, 2 * half:2 * half + 2, first:], ps_s[half][:, :, first:],
                                   ACT.Exp, scale=HD ** -0.5).then_inc(exp_ready, 1)

            def group(n, after=True):
                for u in range(NU):
                    if u + AHEAD < NU:
                        exponentials(n, u + AHEAD)
                    elif after:
                        exponentials(n + 1, u + AHEAD - NU)
                    if u in LAST:
                        j = LAST[u]
                        act.wait_ge(unit_done, n * NU + u + 1)
                        act.wait_ge(o_stored[j % 2], n * 32 + 16 * ((TILES_B - 1 - j) // 2 + 1))
                        act.activation(o_sb[j % 2][:], ps_o[:], ACT.Copy).then_inc(o_ready, 1)

            act.sem_inc(o_ready, 1)
            for k in range(2):
                act.sem_inc(o_stored[k], 16)
            for u in range(AHEAD):
                exponentials(0, u)
            with act.Fori(0, GROUPS - 1) as n:
                group(n)
            group(GROUPS - 1, after=False)

        @block.vector
        def _(dve):
            dve.sem_inc(rows_saved, 16 * TILES_B)
            dve.memset(neg_max[:], 0.0).then_inc(init, 1)
            dve.memset(part[:], LOW).then_inc(init, 1)
            dve.tensor_copy(ident16[:], ident[:]).then_inc(init, 1)
            for k in range(2):
                dve.memset(q_st[k][4 * HD:, :, :].bitcast(F32), 0.0).then_inc(init, 1)
                dve.memset(k_st[k][4 * HD:, :, :].bitcast(F32), 1.0).then_inc(init, 1)
            dve.wait_ge(init, 8)
            with dve.Fori(0, GROUPS) as n:
                for y, item in enumerate(ITEMS):
                    if item[0] == "rows":
                        j = item[1]
                        rows = slice(j * (P // TILES_B), (j + 1) * (P // TILES_B))
                        dve.wait_ge(rows_saved, n * (16 * TILES_B) + 16 * (TILES_B - j))
                        dve.wait_ge(item_psum, n * NI + y + 1)
                        dve.tensor_copy(max_rows[rows], ps_m[y % BANKS][rows, 0:P]).then_inc(item_done, 1)
                        continue
                    _, j, c, segments = item
                    dve.wait_ge(item_psum, n * NI + y + 1)
                    _, i, first, width = segments[0]
                    if width == segments[-1][3]:
                        h = segments[0][0]
                        dve.tensor_reduce(part[:, j, h:h + len(segments), i, c], ps_m[y % BANKS][:, first:first + len(segments) * width].rearrange(
                            "p (a n) -> p a n", n=width), AX_X, ALU.max).then_inc(item_done, 1)
                    else:
                        for h, i, first, width in segments:
                            ins = dve.tensor_reduce(part[:, j, h, i, c:c + 1], ps_m[y % BANKS][:, first:first + width], AX_X, ALU.max)
                        ins.then_inc(item_done, 1)
                    if y not in LAST_CHUNK:
                        continue
                    steps = n * (TILES_B * MAX_STEPS) + (TILES_B - 1 - j) * MAX_STEPS
                    dve.wait_ge(item_done, n * NI + y + 1)
                    dve.tensor_reduce(row_max[:].rearrange("p h i -> p (h i)"), part[:, j].rearrange("p h i c -> p (h i) c"), AX_X, ALU.max).then_inc(max_step, 1)
                    dve.wait_ge(max_step, steps + 1)
                    row = row_max[:].rearrange("p h i -> p (h i)")
                    dve.tensor_scalar(max_h[:], row, -1.0, None, ALU.mult).then_inc(max_step, 1)
                    dve.wait_ge(max_step, steps + 2)
                    dve.tensor_copy(neg_max[:, j, 0], max_h[:].bitcast(F32)).then_inc(max_step, 1)
                    dve.scalar_tensor_tensor(out=neg_max[:, j, 1], in0=row, scalar=-1.0, in1=max_h[:].bitcast(F32),
                                             op0=ALU.mult, op1=ALU.subtract).then_inc(max_step, 1)

        @block.tensor
        def _(pe):
            def scores(n, k, u, half, very_first=False):
                j, kb, first = UNITS[u]
                if kb == 0 and half == 0:
                    pe.wait_ge(rows_landed[j], n * 16 + 16)
                if not very_first:
                    pe.wait_ge(exp_ready, n * (2 * NU) + (2 * u - 1 + half))
                for h in (2 * half, 2 * half + 1):
                    ins = pe.matmul(ps_s[half][:, h % 2, first:], k_st[k][:, h, kb * P:(kb + 1) * P],
                                    q_st[k][:, h, j * TILE + first:(j + 1) * TILE], start=True, stop=True)
                ins.then_inc(score_psum, 1)

            def item(n, k, pair, y):
                if y >= BANKS or not (isinstance(n, int) and n == 0):
                    pe.wait_ge(item_done, n * NI + (y - BANKS + 1))
                if ITEMS[y][0] == "rows":
                    j = ITEMS[y][1]
                    pe.wait_ge(max_step, n * (TILES_B * MAX_STEPS) + (TILES_B - j) * MAX_STEPS)
                    pe.transpose(ps_m[y % BANKS][:, 0:P], neg_max[:].rearrange("p j a n -> p (j a n)"), ident[:]).then_inc(item_psum, 1)
                    return
                _, j, c, segments = ITEMS[y]
                if j == TILES_B - 1 and segments[0][:2] == ((0, 3) if c == j else (0, 0)):
                    pe.wait_ge(landed[k][c], pair * QUARTER + QUARTER)
                for h, i, first, width in segments:
                    query = (j * BLOCKS + i) * P
                    ins = pe.matmul(ps_m[y % BANKS][:, first:first + width], q_st[k][0:KMAX, h, query:query + P],
                                    k_st[k][0:KMAX, h, c * TILE:c * TILE + width], start=True, stop=c < j)
                    if c == j:
                        ins = pe.matmul(ps_m[y % BANKS][:, first + width - P:first + width], ident16[:], mask[:],
                                        start=False, stop=True)
                ins.then_inc(item_psum, 1)

            def times_v(n, k, pair, u):
                j, kb, first = UNITS[u]
                if u == 0:
                    pe.wait_ge(v_landed[k], pair * (16 * TILES_B) + 16 * TILES_B)
                if kb == 0:
                    pe.wait_ge(o_ready, n * TILES_B + (TILES_B - j))
                if kb >= BLOCKS * j:
                    pe.wait_ge(masked, n * (TILES_B * BLOCKS) + (TILES_B - 1 - j) * BLOCKS + kb - BLOCKS * j + 1)
                else:
                    pe.wait_ge(exp_ready, n * (2 * NU) + 2 * (u + 1))
                for h in range(G):
                    ins = pe.matmul(ps_o[h * VW:(h + 1) * VW, first:], v_st[k][:, kb, h * VW:(h + 1) * VW],
                                    probs[u % RING][:, h, first:], start=kb == 0, stop=u in LAST)
                ins.then_inc(unit_done, 1)

            plan = item_plan()

            def group(n, k, pair, after=True):
                for u in range(NU):
                    for piece in range(3):
                        if piece == 2:
                            times_v(n, k, pair, u)
                        elif u + AHEAD < NU:
                            scores(n, k, u + AHEAD, piece)
                        elif after:
                            scores(n + 1, 1 - k, u + AHEAD - NU, piece)
                        for later, y in plan[3 * u + piece]:
                            if not later:
                                item(n, k, pair, y)
                            elif after:
                                item(n + 1, 1 - k, pair + k, y)

            pe.wait_ge(init, 8)
            for y in range(FIRST_ROWS):
                item(0, 0, 0, y)
            for u in range(AHEAD):
                for half in range(2):
                    scores(0, 0, u, half, very_first=u == 0)
            with pe.Fori(0, GROUPS // 2 - 1) as it:
                for k in range(2):
                    group(it * 2 + k, k, it)
            group(GROUPS - 2, 0, GROUPS // 2 - 1)
            group(GROUPS - 1, 1, GROUPS // 2 - 1, after=False)


CENTER = 1.0 / math.e
LOWER = 0.5 - math.log(4.0 / 3.0)
UPPER = 0.5


def route(nc, ident, x_in, o_all, wo, bo, wr, temperature, x1_all, x2T_all, w_all):
    with ExitStack() as ctx:
        def sb(name, shape, dt=F32):
            return ctx.enter_context(nc.sbuf_tensor("ro_" + name, shape, dt))

        def sem(name):
            return ctx.enter_context(nc.semaphore("ro_" + name))

        wo_sb = sb("wo", [P, KT, D])
        bo_row = sb("bo", [P, D])
        wr_sb = sb("wr", [P, KT, E])
        temp = sb("temp", [P, 1])
        temp_r = sb("temp_r", [P, 1])
        num = sb("num", [P, KT, S])
        den = sb("den", [P, KT, S])
        att = sb("att", [P, KT, S])
        x_t = [sb(f"x{k}", [P, BLOCKS, D]) for k in range(2)]
        xb = [sb(f"xb{k}", [P, BLOCKS, D]) for k in range(2)]
        x1 = [sb(f"x1{k}", [P, BLOCKS, D]) for k in range(2)]
        stats = sb("stats", [P, BLOCKS, 6])
        moments = sb("moments", [P, BLOCKS, 2])
        small = sb("small", [P, 4, BLOCKS])
        x2 = [sb(f"x2{k}", [P, BLOCKS, D]) for k in range(2)]
        x2T = [sb(f"x2T{k}", [P, KT, TILE]) for k in range(2)]
        NB = TILES * BLOCKS
        logits = sb("logits", [P, NB, E])
        ps_y = [ctx.enter_context(nc.psum_tensor(f"ro_psy{m}", [P, 2, D], F32)) for m in range(2)]
        ps_T = [ctx.enter_context(nc.psum_tensor(f"ro_psT{m}", [P, TILE], F32)) for m in range(KT)]
        ps_r = ctx.enter_context(nc.psum_tensor("ro_psr", [P, BLOCKS, E], F32))

        consts = sem("consts_landed")
        o_landed = sem("o_landed")
        x_landed = [sem(f"x_landed{k}") for k in range(2)]
        rec_ready = sem("rec_ready")
        att_ready = sem("att_ready")
        xb_ready = sem("xb_ready")
        y_psum = sem("y_psum")
        x1_ready = sem("x1_ready")
        chain_sem = sem("ln_chain")
        passed, passed_sp = sem("passed"), sem("passed_sp")
        var_ready, std_ready, x2_ready = sem("var_ready"), sem("std_ready"), sem("x2_ready")
        xT_psum = sem("xT_psum")
        xT_ready = sem("xT_ready")
        r_psum = sem("r_psum")
        r_ready = sem("r_ready")
        x1_stored = [sem(f"x1_stored{k}") for k in range(2)]
        xT_stored = [sem(f"xT_stored{k}") for k in range(2)]
        step_sem = sem("step")
        z_ready, exps = sem("z_ready"), sem("exps")
        w_stored = sem("w_stored")
        WEIGH_STEPS = E + 36
        z, den1, inh, zone, dist, w, fb, rest, top1, top2, order = (
            sb(name, [P, NB, E]) for name in "z den1 inh zone dist w fb rest top1 top2 order".split())
        total, none = sb("total", [P, NB]), sb("none", [P, NB])
        O_DMAS = 2 * H

        block = ctx.enter_context(nc.Block())

        @block.sync
        def _(sp):
            sp.dma_start(wo_sb[:], wo.rearrange("(k p) n -> p k n", p=P)).then_inc(consts, 16)
            sp.dma_start(bo_row[:], bo.rearrange("(a n) -> a n", a=1).to_broadcast([P, D])).then_inc(consts, 16)
            sp.dma_start(wr_sb[:], wr.rearrange("(k p) n -> p k n", p=P)).then_inc(consts, 16)
            sp.dma_start(temp[:], temperature.rearrange("(a n) -> a n", a=1).to_broadcast([P, 1])).then_inc(consts, 16)
            for k in range(2):
                sp.sem_inc(x1_stored[k], 16)
                sp.sem_inc(xT_stored[k], 16)
            with sp.Fori(0, B) as b:
                sp.wait_ge(att_ready, b * TILES_B + TILES_B)
                for h in range(H):
                    row = (h * HD) % P
                    for tile, skip in ((num, 0), (den, HD)):
                        sp.dma_start(tile[row:row + HD, h * HD // P, :],
                                     o_all[bass.ds(b * (H * VW) + (h * VW + skip), HD), :]).then_inc(o_landed, 16)
                for i in range(TILES_B):
                    k = i % 2
                    first = bass.ds(b * S + i * TILE, TILE)
                    sp.wait_ge(x1_ready, b * (2 * TILES_B) + (2 * i + 6))
                    sp.dma_start(x1_all[first, :].rearrange("(j p) d -> p j d", p=P), x1[k][:]).then_inc(x1_stored[k], 16)
                    wait_apart(sp, xT_ready, b * (KT * TILES_B) + KT * (i + 1), passed_sp)
                    sp.dma_start(x2T_all[:, first].rearrange("(m p) n -> p m n", p=P), x2T[k][:]).then_inc(xT_stored[k], 16)
            for k in range(2):
                sp.wait_ge(x1_stored[k], 16 * (TILES // 2 + 1))
                sp.wait_ge(xT_stored[k], 16 * (TILES // 2 + 1))

        @block.gpsimd
        def _(pool):
            pool.wait_ge(consts, 16 * 4)
            with pool.Fori(0, B) as b:
                for i in range(TILES_B):
                    k = i % 2
                    pool.wait_ge(x1_ready, b * (2 * TILES_B) + (2 * i + 2))
                    pool.dma_start(x_t[k][:], x_in[bass.ds(b * S + i * TILE, TILE), :].rearrange(
                        "(j p) d -> p j d", p=P)).then_inc(x_landed[k], 16)
                    pool.wait_ge(x_landed[k], b * 32 + 16 * (i // 2 + 1))
                    pool.tensor_tensor(xb[k][:], x_t[k][:], bo_row[:].unsqueeze(1).to_broadcast([P, BLOCKS, D]),
                                       ALU.add).then_inc(xb_ready, 1)
            pool.wait_ge(step_sem, WEIGH_STEPS)
            pool.dma_start(w_all.rearrange("(n p) e -> p n e", p=P), w[:]).then_inc(w_stored, 16)
            pool.wait_ge(w_stored, 16)

        @block.scalar
        def _(act):
            with act.Fori(0, B) as b:
                for i in range(TILES_B):
                    k = i % 2
                    t = b * TILES_B + i
                    act.wait_ge(var_ready, t + 1)
                    act.activation(small[:, 1, :], small[:, 0, :], ACT.Sqrt).then_inc(std_ready, 1)
                    act.wait_ge(xT_stored[k], b * 32 + 16 * (i // 2 + 1))
                    for m in range(KT):
                        act.wait_ge(xT_psum, t * KT + m + 1)
                        act.activation(x2T[k][:, m], ps_T[m][:], ACT.Identity).then_inc(xT_ready, 1)
            act.wait_ge(z_ready, 1)
            act.activation(z[:], z[:], ACT.Exp, scale=-1.0).then_inc(exps, 1)
            act.wait_ge(z_ready, 2)
            act.activation(w[:], dist[:], ACT.Exp, scale=-1.0 / 0.1).then_inc(exps, 1)
            act.activation(fb[:], dist[:], ACT.Exp, scale=-1.0 / 0.3).then_inc(exps, 1)

        @block.tensor
        def _(pe):
            pe.wait_ge(consts, 16 * 4)
            with pe.Fori(0, B) as b:
                for i in range(TILES_B):
                    k = i % 2
                    t = b * TILES_B + i
                    pe.wait_ge(att_ready, t + TILES_B + 1)
                    for m in range(2):
                        pe.wait_ge(x1_ready, t * 2 + m + 3)
                        for j in range(2):
                            for c in range(KT):
                                first = i * TILE + (2 * m + j) * P
                                ins = pe.matmul(ps_y[m][:, j], att[:, c, first:first + P], wo_sb[:, c],
                                                start=c == 0, stop=c == KT - 1)
                        ins.then_inc(y_psum, 1)
                    pe.wait_ge(x2_ready, t * BLOCKS + BLOCKS)
                    for m in range(KT):
                        for j in range(BLOCKS):
                            ins = pe.transpose(ps_T[m][:, j * P:(j + 1) * P], x2[k][:, j, m * P:(m + 1) * P], ident[:])
                        ins.then_inc(xT_psum, 1)
                    pe.wait_ge(xT_ready, t * KT + KT)
                    pe.wait_ge(r_ready, t + 1)
                    for j in range(BLOCKS):
                        for c in range(KT):
                            ins = pe.matmul(ps_r[:, j], x2T[k][:, c, j * P:(j + 1) * P], wr_sb[:, c],
                                            start=c == 0, stop=c == KT - 1)
                    ins.then_inc(r_psum, 1)

        @block.vector
        def _(dve):
            chain = Tally(chain_sem, LN_CHAIN)
            dve.sem_inc(att_ready, TILES_B)
            dve.sem_inc(x1_ready, 4)
            dve.sem_inc(r_ready, 1)
            with dve.Fori(0, B) as b:
                dve.wait_ge(o_landed, b * (16 * O_DMAS) + 16 * O_DMAS)
                for i in range(TILES_B):
                    k = i % 2
                    t = b * TILES_B + i
                    cols = slice(i * TILE, (i + 1) * TILE)
                    dve.reciprocal(den[:, :, cols], den[:, :, cols]).then_inc(rec_ready, 1)
                    dve.wait_ge(rec_ready, t + 1)
                    dve.tensor_tensor(att[:, :, cols], num[:, :, cols], den[:, :, cols], ALU.mult).then_inc(att_ready, 1)
                for i in range(TILES_B):
                    k = i % 2
                    t = b * TILES_B + i
                    dve.wait_ge(xb_ready, t + 1)
                    dve.wait_ge(x1_stored[k], b * 32 + 16 * (i // 2 + 1))
                    for m in range(2):
                        dve.wait_ge(y_psum, t * 2 + m + 1)
                        dve.tensor_tensor(x1[k][:, 2 * m:2 * m + 2], ps_y[m][:], xb[k][:, 2 * m:2 * m + 2],
                                          ALU.add).then_inc(x1_ready, 1)
                    dve.wait_ge(x1_ready, t * 2 + 6)
                    chain.start()
                    layer_norm(dve, chain, t, passed, x1[k], stats, moments, small, x2[k], var_ready, std_ready, x2_ready)
                    chain.end()
                    dve.wait_ge(r_psum, t + 1)
                    dve.tensor_copy(logits[:, bass.ds(t * BLOCKS, BLOCKS), :], ps_r[:]).then_inc(r_ready, 1)


            step = Tally(step_sem, WEIGH_STEPS)

            def do(instruction):
                step.up(instruction)
                step.wait(dve, 0)

            def over(column):
                return column.unsqueeze(2).to_broadcast([P, NB, E])

            tt, ts = dve.tensor_tensor, dve.tensor_scalar
            dve.wait_ge(r_ready, TILES + 1)
            for e in range(E):
                do(dve.memset(order[:, :, e], float(E - e)))
            do(dve.reciprocal(temp_r[:], temp[:]))
            ts(z[:], logits[:], temp_r[:, 0:1], None, ALU.mult).then_inc(z_ready, 1)
            dve.wait_ge(exps, 1)
            do(ts(den1[:], z[:], 1.0, None, ALU.add))
            do(dve.reciprocal(inh[:], den1[:]))
            do(ts(zone[:], inh[:], LOWER, None, ALU.is_ge))
            do(dve.scalar_tensor_tensor(out=zone[:], in0=inh[:], scalar=UPPER, in1=zone[:], op0=ALU.is_le, op1=ALU.mult))
            do(ts(inh[:], inh[:], CENTER, None, ALU.subtract))
            dve.scalar_tensor_tensor(out=dist[:], in0=inh[:], scalar=-1.0, in1=inh[:], op0=ALU.mult, op1=ALU.max).then_inc(z_ready, 1)
            dve.wait_ge(exps, 3)
            do(tt(w[:], w[:], zone[:], ALU.mult))
            do(dve.tensor_reduce(total[:], w[:], AX_X, ALU.add))
            do(ts(none[:], total[:], 1e-8, None, ALU.is_lt))
            do(dve.tensor_copy(rest[:], fb[:]))
            for mask in (top1, top2):
                do(dve.tensor_reduce(total[:], rest[:], AX_X, ALU.max))
                do(tt(mask[:], rest[:], over(total[:]), ALU.is_equal))
                do(tt(mask[:], mask[:], order[:], ALU.mult))
                do(dve.tensor_reduce(total[:], mask[:], AX_X, ALU.max))
                do(tt(mask[:], mask[:], over(total[:]), ALU.is_equal))
                do(dve.scalar_tensor_tensor(out=rest[:], in0=mask[:], scalar=-10.0, in1=rest[:], op0=ALU.mult, op1=ALU.add))
            do(tt(top1[:], top1[:], top2[:], ALU.add))
            do(tt(fb[:], fb[:], top1[:], ALU.mult))

            def normalise(x):
                do(dve.tensor_reduce(total[:], x[:], AX_X, ALU.add))
                do(ts(total[:], total[:], 1e-8, None, ALU.max))
                do(dve.reciprocal(total[:], total[:]))
                do(tt(x[:], x[:], over(total[:]), ALU.mult))

            normalise(fb)
            do(tt(fb[:], fb[:], over(none[:]), ALU.mult))
            do(ts(none[:], none[:], -1.0, 1.0, ALU.mult, ALU.add))
            do(tt(w[:], w[:], over(none[:]), ALU.mult))
            do(tt(w[:], w[:], fb[:], ALU.add))
            normalise(w)
            step.end()


SLICES = E * I // P
PASSES = ((0, 0), (0, 1), (1, 0))


def experts(nc, x2T_all, w_all, x1_all, wg, wu, wd, out):
    with ExitStack() as ctx:
        def sb(name, shape, dt=F32):
            return ctx.enter_context(nc.sbuf_tensor("ex_" + name, shape, dt))

        def sem(name):
            return ctx.enter_context(nc.semaphore("ex_" + name))

        wg_sb = [sb(f"wg{n}", [P, KT, E * I], F32R) for n in range(2)]
        wu_sb = [sb(f"wu{n}", [P, KT, E * I], F32R) for n in range(2)]
        wd_sb = [sb(f"wd{n}", [P, SLICES, D], F32R) for n in range(2)]
        x2_f = [sb(f"x2f{k}", [P, KT, TILE]) for k in range(2)]
        x2_s = [[sb(f"x2s{k}{n}", [P, KT, TILE], F32R) for n in range(2)] for k in range(2)]
        w_row = [sb(f"wrow{k}", [P, TILE, E]) for k in range(2)]
        stage = [w_row[k][:].rearrange("p n e -> p (n e)")[:, 0:E * I] for k in range(2)]
        silu = [sb(f"silu{k}", [P, TILE]) for k in range(2)]
        up_w = sb("up_w", [P, TILE])
        h_f = sb("h_f", [P, TILE])
        h_s = [[sb(f"h{k}{n}", [P, TILE], F32R) for n in range(2)] for k in range(2)]
        x1_t = [sb(f"x1{k}", [P, BLOCKS, D]) for k in range(2)]
        out_t = [sb(f"out{k}", [P, BLOCKS, D]) for k in range(2)]
        ps_g = [ctx.enter_context(nc.psum_tensor(f"ex_psg{m}", [P, TILE], F32)) for m in range(2)]
        ps_u = [ctx.enter_context(nc.psum_tensor(f"ex_psu{m}", [P, TILE], F32)) for m in range(2)]
        ps_d = [ctx.enter_context(nc.psum_tensor(f"ex_psd{m}", [P, TILE], F32)) for m in range(BLOCKS)]

        staged = [sem(f"staged{k}") for k in range(2)]
        high_ready = sem("high_ready")
        low_ready = sem("low_ready")
        x2_landed = [sem(f"x2_landed{k}") for k in range(2)]
        w_landed = [sem(f"w_landed{k}") for k in range(2)]
        x1_landed = [sem(f"x1_landed{k}") for k in range(2)]
        passed = sem("passed")
        x2_split = sem("x2_split")
        gu_psum = sem("gu_psum")
        silu_ready = sem("silu_ready")
        up_ready = sem("up_ready")
        h_ready = sem("h_ready")
        h_high = sem("h_high")
        h_low = sem("h_low")
        down_done = sem("down_done")
        y_ready = sem("y_ready")
        out_stored = [sem(f"out_stored{k}") for k in range(2)]

        chunks = []
        for w, tiles in ((wg, wg_sb), (wu, wu_sb)):
            for c in range(KT):
                chunks.append((w[:, c * P:(c + 1) * P, :].rearrange("e p i -> p e i"), E, [x[:, c] for x in tiles]))
        for c in range(2):
            half = SLICES // 2
            src = wd.rearrange("e (s p) d -> p (e s) d", p=P)[:, c * half:(c + 1) * half]
            chunks.append((src, half, [x[:, c * half:(c + 1) * half].rearrange("p s d -> p (s d)") for x in wd_sb]))

        block = ctx.enter_context(nc.Block())

        @block.sync
        def _(sp):
            def load(t, k):
                first = bass.ds(t * TILE, TILE)
                sp.dma_start(x2_f[k][:], x2T_all[:, first].rearrange("(m p) n -> p m n", p=P)).then_inc(x2_landed[k], 16)
                sp.dma_start(x1_t[k][:], x1_all[first, :].rearrange("(j p) d -> p j d", p=P)).then_inc(x1_landed[k], 16)

            def load_w(t, k):
                sp.dma_start(w_row[k][:].rearrange("p n e -> p (n e)"),
                             w_all[bass.ds(t * TILE, TILE), :].rearrange("(a n) e -> a (n e)", a=1).to_broadcast([P, TILE * E])).then_inc(w_landed[k], 16)

            def store(t, k):
                sp.wait_ge(y_ready, t * BLOCKS + 2 * BLOCKS)
                sp.dma_start(out[bass.ds(t * TILE, TILE), :].rearrange("(j p) d -> p j d", p=P), out_t[k][:]).then_inc(out_stored[k], 16)

            for n, (src, parts, _) in enumerate(chunks):
                if n >= 2:
                    sp.wait_ge(low_ready, n - 1)
                sp.dma_start(stage[n % 2].rearrange("p (a b) -> p a b", a=parts), src).then_inc(staged[n % 2], 16)
            for k in range(2):
                load(k, k)
                sp.wait_ge(low_ready, len(chunks) - 1 + k)
                load_w(k, k)
            with sp.Fori(0, TILES // 2 - 1) as it:
                for k in range(2):
                    store(it * 2 + k, k)
                    load(it * 2 + (k + 2), k)
                    load_w(it * 2 + (k + 2), k)
            for k in range(2):
                store(TILES - 2 + k, k)
            for k in range(2):
                sp.wait_ge(out_stored[k], 16 * (TILES // 2 + 1))

        @block.gpsimd
        def _(pool):
            with pool.Fori(0, TILES // 2) as it:
                for k in range(2):
                    t = it * 2 + k
                    pool.wait_ge(x2_landed[k], it * 16 + 16)
                    wait_apart(pool, gu_psum, t * SLICES + SLICES, passed)
                    pool.tensor_copy(x2_s[k][0][:], x2_f[k][:]).then_inc(x2_split, 1)
                    pool.wait_ge(x2_split, t * 2 + 1)
                    pool.tensor_tensor(x2_s[k][1][:], x2_f[k][:], x2_s[k][0][:].bitcast(F32), ALU.subtract).then_inc(x2_split, 1)

        @block.scalar
        def _(act):
            with act.Fori(0, TILES) as t:
                for s in range(SLICES):
                    act.wait_ge(gu_psum, t * SLICES + (2 * SLICES + s + 1))
                    act.activation(silu[s % 2][:], ps_g[s % 2][:], ACT.Silu).then_inc(silu_ready, 1)

        @block.vector
        def _(dve):
            dve.sem_inc(y_ready, BLOCKS)
            for k in range(2):
                dve.sem_inc(out_stored[k], 16)
            for n, (_, _, halves) in enumerate(chunks):
                dve.wait_ge(staged[n % 2], 16 * (n // 2 + 1))
                dve.tensor_copy(halves[0], stage[n % 2]).then_inc(high_ready, 1)
                dve.wait_ge(high_ready, n + 1)
                dve.tensor_tensor(halves[1], stage[n % 2], halves[0].bitcast(F32), ALU.subtract).then_inc(low_ready, 1)
            with dve.Fori(0, TILES // 2) as it:
                for k in range(2):
                    t = it * 2 + k
                    dve.wait_ge(w_landed[k], it * 16 + 16)
                    for s in range(SLICES):
                        dve.wait_ge(gu_psum, t * SLICES + (2 * SLICES + s + 1))
                        dve.tensor_tensor(up_w[:], ps_u[s % 2][:], w_row[k][:, :, s * P // I], ALU.mult).then_inc(up_ready, 1)
                        dve.wait_ge(up_ready, t * SLICES + (s + 1))
                        dve.wait_ge(silu_ready, t * SLICES + (s + 1))
                        dve.tensor_tensor(h_f[:], up_w[:], silu[s % 2][:], ALU.mult).then_inc(h_ready, 1)
                        dve.wait_ge(h_ready, t * SLICES + (s + 1))
                        dve.wait_ge(down_done, t * SLICES + (s + 1))
                        dve.tensor_copy(h_s[s % 2][0][:], h_f[:]).then_inc(h_high, 1)
                        dve.wait_ge(h_high, t * SLICES + (s + 1))
                        dve.tensor_tensor(h_s[s % 2][1][:], h_f[:], h_s[s % 2][0][:].bitcast(F32), ALU.subtract).then_inc(h_low, 1)
                    dve.wait_ge(down_done, t * SLICES + (SLICES + 2))
                    dve.wait_ge(x1_landed[k], it * 16 + 16)
                    dve.wait_ge(out_stored[k], it * 16 + 16)
                    for j in range(BLOCKS):
                        dve.tensor_tensor(out_t[k][:, j], ps_d[j][:, 0:D], x1_t[k][:, j], ALU.add).then_inc(y_ready, 1)

        @block.tensor
        def _(pe):
            def gate_up(t, k, s, free=True):
                if s == 0:
                    pe.wait_ge(x2_split, t * 2 + 2)
                if free:
                    pe.wait_ge(h_ready, t * SLICES + (s - 1))
                for ps, w in ((ps_g[s % 2], wg_sb), (ps_u[s % 2], wu_sb)):
                    for c in range(KT):
                        for n, (wh, xh) in enumerate(PASSES):
                            ins = pe.matmul(ps[:], w[wh][:, c, s * P:(s + 1) * P], x2_s[k][xh][:, c],
                                            start=c == 0 and n == 0, stop=c == KT - 1 and n == len(PASSES) - 1)
                ins.then_inc(gu_psum, 1)

            def down(t, s):
                pe.wait_ge(h_low, t * SLICES + (s + 1))
                for j in range(BLOCKS):
                    if s == 0:
                        pe.wait_ge(y_ready, t * BLOCKS + BLOCKS)
                    for n, (wh, hh) in enumerate(PASSES):
                        ins = pe.matmul(ps_d[j][:, 0:D], h_s[s % 2][hh][:, j * P:(j + 1) * P], wd_sb[wh][:, s],
                                        start=s == 0 and n == 0, stop=s == SLICES - 1 and n == len(PASSES) - 1)
                ins.then_inc(down_done, 1)

            def tile(t, k, after=True):
                for s in range(SLICES):
                    if s + 2 < SLICES:
                        gate_up(t, k, s + 2)
                    elif after:
                        gate_up(t + 1, 1 - k, s + 2 - SLICES)
                    down(t, s)

            pe.sem_inc(gu_psum, 2 * SLICES)
            pe.sem_inc(down_done, 2)
            pe.wait_ge(low_ready, len(chunks))
            for s in range(2):
                gate_up(0, 0, s, free=False)
            with pe.Fori(0, TILES // 2 - 1) as it:
                for k in range(2):
                    tile(it * 2 + k, k)
            tile(TILES - 2, 0)
            tile(TILES - 1, 1, after=False)


def build(nc, x, wq, bq, wk, bk, wv, bv, wo, bo, wg, wu, wd, wr, temperature, out):
    def scratch(name, shape):
        return nc.dram_tensor(name, shape, F32, kind="Internal").ap()

    q_hi, q_lo, k_hi, k_lo = (scratch(name, (B * D, S)) for name in ("q_hi", "q_lo", "k_hi", "k_lo"))
    v_all = scratch("v_all", (B * GROUPS_B, S, G * VW))
    o_all = scratch("o_all", (B * H * VW, S))
    m_all = scratch("m_all", (GROUPS * P, P))
    x1_all = scratch("x1_all", (B * S, D))
    x2T_all = scratch("x2T_all", (D, B * S))
    w_all = scratch("w_all", (B * S, E))
    x_in, y_out = x.rearrange("b s d -> (b s) d"), out.rearrange("b s d -> (b s) d")
    with ExitStack() as ctx:
        ident = ctx.enter_context(nc.sbuf_tensor("ident", [P, P], F32))
        made = ctx.enter_context(nc.semaphore("ident_made"))
        with nc.Block() as block:
            @block.gpsimd
            def _(pool):
                pool.memset(ident[:], 0.0).then_inc(made, 1)
                pool.wait_ge(made, 1)
                pool.affine_select(out=ident[:], in_=ident[:], compare_op=ALU.not_equal, fill=1.0, base=0,
                                   pattern=[[-1, P]], channel_multiplier=1).then_inc(made, 1)
                pool.wait_ge(made, 2)
        project(nc, ident, x_in, wq, bq, wk, bk, wv, bv, q_hi, q_lo, k_hi, k_lo, v_all)
        attend(nc, ident, q_hi, q_lo, k_hi, k_lo, v_all, m_all, o_all)
        route(nc, ident, x_in, o_all, wo, bo, wr, temperature, x1_all, x2T_all, w_all)
        experts(nc, x2T_all, w_all, x1_all, wg, wu, wd, y_out)


_INS = ["L0_attn_x", "L0_attn_wq", "L0_attn_bq", "L0_attn_wk", "L0_attn_bk", "L0_attn_wv", "L0_attn_bv",
        "L0_attn_wo", "L0_attn_bo", "L0_ffn_Wg", "L0_ffn_Wu", "L0_ffn_Wd", "L0_ffn_Wr", "L0_ffn_temperature"]


def kernel(**inputs):
    import numpy as _np
    import concourse.bacc as _bacc
    from concourse import mybir as _mybir
    from concourse.bass_utils import run_bass_kernel_spmd as _run

    nc = _bacc.Bacc("TRN2", target_bir_lowering=False, num_devices=1)
    arrays, args = {}, []
    for name in _INS:
        a = _np.ascontiguousarray(inputs[name])
        arrays[f"in_{name}_dram"] = a
        args.append(nc.dram_tensor(f"in_{name}_dram", a.shape, _mybir.dt.from_np(a.dtype), kind="ExternalInput").ap())
    args.append(nc.dram_tensor("out_0_dram", (B, S, D), _mybir.dt.float32, kind="ExternalOutput").ap())
    build(nc, *args)
    r = _run(nc, [arrays], core_ids=[0])
    return r.results[0]["out_0_dram"]
```

```python
import math
from contextlib import ExitStack

import concourse.bass as bass
from concourse import mybir

F32 = mybir.dt.float32
F32R = mybir.dt.float32r
BF16 = mybir.dt.bfloat16
ALU = mybir.AluOpType
ACT = mybir.ActivationFunctionType
AX_X = mybir.AxisListType.X

P = 128
B, S, D = 4, 2048, 256
H, HD = 16, 16
E, I = 8, 256
KT = D // P
TILE = 512
BLOCKS = TILE // P
TILES_B = S // TILE
TILES = B * TILES_B
G = 4
GROUPS_B = H // G
GROUPS = B * GROUPS_B
VW = 2 * HD
EPS = 1e-5
LOW = -3.0e38


def wait_apart(engine, sem, value, passed):
    engine.wait_ge(sem, value)
    engine.sem_inc(passed, 1)


class Tally:

    def __init__(self, sem, per_tile):
        self.sem, self.per_tile, self.count = sem, per_tile, 0

    def start(self):
        self.count = 0

    def up(self, instruction):
        instruction.then_inc(self.sem, 1)
        self.count += 1

    def wait(self, engine, tile):
        engine.wait_ge(self.sem, tile * self.per_tile + self.count)

    def end(self):
        assert self.count == self.per_tile, (self.count, self.per_tile)


def ln_variance(dve, chain, tile, passed, x, stats, moments, small, var_ready):
    for j in range(BLOCKS):
        chain.up(dve.bn_stats(stats[:, j, :], x[:, j, :]))
    wait_apart(dve, chain.sem, tile * chain.per_tile + chain.count, passed)
    for j in range(BLOCKS):
        chain.up(dve.bn_aggr(moments[:, j, :], stats[:, j, :]))
    chain.wait(dve, tile)
    dve.tensor_scalar(small[:, 0, :], moments[:, :, 1], EPS, None, ALU.add).then_inc(var_ready, 1)


def ln_root(dve, chain, tile, small, var_ready, std_ready):
    var, std, rec, tmp = (small[:, n, :] for n in range(4))
    dve.wait_ge(var_ready, tile + 1)
    dve.wait_ge(std_ready, tile + 1)
    chain.up(dve.reciprocal(rec, std))
    chain.wait(dve, tile)
    chain.up(dve.tensor_tensor(tmp, var, rec, ALU.mult))
    chain.wait(dve, tile)
    chain.up(dve.tensor_tensor(std, std, tmp, ALU.add))
    chain.wait(dve, tile)
    chain.up(dve.tensor_scalar(tmp, std, 0.5, None, ALU.mult))
    chain.wait(dve, tile)
    chain.up(dve.reciprocal(rec, tmp))
    chain.wait(dve, tile)


def ln_scale(dve, x, moments, small, xn, xn_ready):
    for j in range(BLOCKS):
        dve.tensor_scalar(xn[:, j, :], x[:, j, :], moments[:, j, 0:1], small[:, 2, j:j + 1],
                          ALU.subtract, ALU.mult).then_inc(xn_ready, 1)


LN_CHAIN = 4 + 4 + 5
PASSES = ((0, 0), (0, 1), (1, 0))


def project(nc, ident, x_in, wq, bq, wk, bk, wv, bv, q_hi, q_lo, k_hi, k_lo, v_all):
    with ExitStack() as ctx:
        def sb(name, shape, dt=F32):
            return ctx.enter_context(nc.sbuf_tensor("pr_" + name, shape, dt))

        def sem(name):
            return ctx.enter_context(nc.semaphore("pr_" + name))

        w_sb = sb("w", [P, 3, KT, D])
        w_s = [sb(f"w_s{n}", [P, 3, KT, D], F32R) for n in range(2)]
        bias_col = sb("bias_col", [P, 2, KT])
        bv_row = sb("bv_row", [P, 2, D])
        x_t = [sb(f"x{k}", [P, BLOCKS, D]) for k in range(2)]
        stats = sb("stats", [P, BLOCKS, 6])
        moments = sb("moments", [P, BLOCKS, 2])
        small = sb("small", [P, 4, BLOCKS])
        xn = [sb(f"xn{k}", [P, BLOCKS, D]) for k in range(2)]
        xnT = [sb(f"xnT{k}", [P, KT, TILE]) for k in range(2)]
        xnT_s = [[sb(f"xnT_s{k}{n}", [P, KT, TILE], F32R) for n in range(2)] for k in range(2)]
        qk_f = [sb(f"qk_f{k}", [P, 2 * KT, TILE]) for k in range(2)]
        qk_h = [sb(f"qk_h{k}", [P, 2 * KT, TILE], F32R) for k in range(2)]
        qk_l = [sb(f"qk_l{k}", [P, 2 * KT, TILE], F32R) for k in range(2)]
        v_t = [sb(f"v{k}", [P, BLOCKS, H, VW]) for k in range(2)]
        ps_T = [ctx.enter_context(nc.psum_tensor(f"pr_psT{m}", [P, TILE], F32)) for m in range(KT)]
        ps_qk = [ctx.enter_context(nc.psum_tensor(f"pr_psqk{m}", [P, TILE], F32)) for m in range(4)]
        ps_v = [ctx.enter_context(nc.psum_tensor(f"pr_psv{m}", [P, 2, D], F32)) for m in range(2)]

        consts = sem("consts_landed")
        ones = sem("v_ones")
        x_landed = [sem(f"x_landed{k}") for k in range(2)]
        chain_sem = sem("ln_chain")
        passed = sem("passed")
        var_ready, std_ready, xn_ready = sem("var_ready"), sem("std_ready"), sem("xn_ready")
        xT_psum = sem("xT_psum")
        xT_ready = sem("xT_ready")
        xT_high = sem("xT_high")
        xT_low = sem("xT_low")
        w_high, w_low = sem("w_high"), sem("w_low")
        qk_psum = sem("qk_psum")
        v_psum = sem("v_psum")
        qk_full = sem("qk_full")
        hi_ready = sem("hi_ready")
        lo_ready = sem("lo_ready")
        v_ready = sem("v_ready")
        stored = [sem(f"stored{k}") for k in range(2)]

        STORES = 4 + BLOCKS
        block = ctx.enter_context(nc.Block())

        @block.sync
        def _(sp):
            for n, w in enumerate((wq, wk, wv)):
                sp.dma_start(w_sb[:, n], w.rearrange("(k p) n -> p k n", p=P)).then_inc(consts, 16)
            for n, bias in enumerate((bq, bk)):
                sp.dma_start(bias_col[:, n], bias.rearrange("(k p) -> p k", p=P),
                             allow_slow_non_contiguous=True).then_inc(consts, 16)
            for n in range(2):
                sp.dma_start(bv_row[:, n], bv.rearrange("(a n) -> a n", a=1).to_broadcast([P, D])).then_inc(consts, 16)
            for k in range(2):
                sp.sem_inc(stored[k], 16 * STORES)
                sp.dma_start(x_t[k][:], x_in[k * TILE:(k + 1) * TILE, :].rearrange(
                    "(j p) d -> p j d", p=P)).then_inc(x_landed[k], 16)

            def store(b, t, j, k):
                sp.wait_ge(lo_ready, t * 4 + 4)
                sp.wait_ge(v_ready, t * 2 + 4)
                rows, cols = bass.ds(b * D, D), bass.ds(j * (2 * TILE) + k * TILE, TILE)
                for dram, tile, m in ((q_hi, qk_h, 0), (q_lo, qk_l, 0), (k_hi, qk_h, 2), (k_lo, qk_l, 2)):
                    sp.dma_start(dram[rows, cols].rearrange("(m p) n -> p m n", p=P),
                                 tile[k][:, m:m + 2].bitcast(F32)).then_inc(stored[k], 16)
                for i in range(BLOCKS):
                    sp.dma_start(
                        v_all[bass.ds(b * GROUPS_B, GROUPS_B),
                              bass.ds(j * (2 * TILE) + (k * TILE + i * P), P), :].rearrange("g p n -> p g n"),
                        v_t[k][:, i].rearrange("p (g h) n -> p g (h n)", h=G)).then_inc(stored[k], 16)

            def pair(b, j, loads):
                for k in range(2):
                    t = b * TILES_B + j * 2 + k
                    if k < loads:
                        sp.wait_ge(xn_ready, t * BLOCKS + 2 * BLOCKS)
                        sp.dma_start(x_t[1 - k][:], x_in[bass.ds(b * S + j * (2 * TILE) + (k + 3) * TILE, TILE), :].rearrange(
                            "(j p) d -> p j d", p=P)).then_inc(x_landed[1 - k], 16)
                    store(b, t, j, k)

            sp.wait_ge(xn_ready, BLOCKS)
            sp.dma_start(x_t[0][:], x_in[2 * TILE:3 * TILE, :].rearrange("(j p) d -> p j d", p=P)).then_inc(x_landed[0], 16)
            with sp.Fori(0, B - 1) as b:
                with sp.Fori(0, TILES_B // 2) as j:
                    pair(b, j, 2)
            for j in range(TILES_B // 2):
                pair(B - 1, j, 1 - j)
            for k in range(2):
                sp.wait_ge(stored[k], 16 * STORES * (TILES // 2 + 1))

        @block.gpsimd
        def _(pool):
            for k in range(2):
                pool.memset(v_t[k][:], 1.0).then_inc(ones, 1)

            def split(t, k):
                for m in range(KT):
                    pool.wait_ge(xT_high, t * KT + m + 1)
                    pool.tensor_tensor(xnT_s[k][1][:, m], xnT[k][:, m], xnT_s[k][0][:, m].bitcast(F32),
                                       ALU.subtract).then_inc(xT_low, 1)

            def tile(t, k, nth, after):
                pool.wait_ge(stored[k], nth * (16 * STORES) + 16 * STORES)
                for m in range(4):
                    pool.wait_ge(hi_ready, t * 4 + m + 1)
                    pool.tensor_tensor(qk_l[k][:, m], qk_f[k][:, m], qk_h[k][:, m].bitcast(F32),
                                       ALU.subtract).then_inc(lo_ready, 1)
                    if m == 1 and after:
                        split(t + 1, 1 - k)

            split(0, 0)
            with pool.Fori(0, TILES // 2 - 1) as it:
                for k in range(2):
                    tile(it * 2 + k, k, it, True)
            for k in range(2):
                tile(TILES - 2 + k, k, TILES // 2 - 1, k == 0)

        @block.scalar
        def _(act):
            def root(t):
                act.wait_ge(var_ready, t + 1)
                act.activation(small[:, 1, :], small[:, 0, :], ACT.Sqrt).then_inc(std_ready, 1)

            def transposed(t, k):
                for m in range(KT):
                    act.wait_ge(xT_psum, t * KT + m + 1)
                    act.activation(xnT[k][:, m], ps_T[m][:], ACT.Identity).then_inc(xT_ready, 1)

            def tile(t, k, nth, after, later):
                act.wait_ge(stored[k], nth * (16 * STORES) + 16 * STORES)
                for m in range(4):
                    act.wait_ge(qk_psum, t * 4 + m + 1)
                    act.activation(qk_f[k][:, m], ps_qk[m][:], ACT.Identity,
                                   bias=bias_col[:, m // 2, m % 2:m % 2 + 1]).then_inc(qk_full, 1)
                    if m == 1 and after:
                        transposed(t + 1, 1 - k)
                if later:
                    root(t + 2)

            act.sem_inc(qk_full, 4)
            act.wait_ge(consts, 16 * 7)
            root(0)
            transposed(0, 0)
            root(1)
            with act.Fori(0, TILES // 2 - 1) as it:
                for k in range(2):
                    tile(it * 2 + k, k, it, True, True)
            for k in range(2):
                tile(TILES - 2 + k, k, TILES // 2 - 1, k == 0, False)

        @block.vector
        def _(dve):
            chain = Tally(chain_sem, LN_CHAIN)

            def normalise(t, k, nth):
                dve.wait_ge(x_landed[k], nth * 16 + 16)
                chain.start()
                ln_variance(dve, chain, t, passed, x_t[k], stats, moments, small, var_ready)
                ln_root(dve, chain, t, small, var_ready, std_ready)
                chain.end()
                ln_scale(dve, x_t[k], moments, small, xn[k], xn_ready)

            def split(t, k):
                for m in range(KT):
                    dve.wait_ge(xT_ready, t * KT + m + 1)
                    dve.tensor_copy(xnT_s[k][0][:, m], xnT[k][:, m]).then_inc(xT_high, 1)

            def tile(t, k, nth, after, later):
                dve.wait_ge(stored[k], nth * (16 * STORES) + 16 * STORES)
                for m in range(4):
                    dve.wait_ge(qk_full, t * 4 + m + 5)
                    dve.tensor_copy(qk_h[k][:, m], qk_f[k][:, m]).then_inc(hi_ready, 1)
                    if m == 1 and after:
                        split(t + 1, 1 - k)
                if later:
                    normalise(t + 2, k, nth + 1)
                for m in range(2):
                    dve.wait_ge(v_psum, t * 2 + m + 1)
                    dve.tensor_tensor(
                        v_t[k][:, 2 * m:2 * m + 2, :, 0:HD].rearrange("p j h c -> p (j h) c"),
                        ps_v[m][:].rearrange("p j (h c) -> p (j h) c", c=HD),
                        bv_row[:].rearrange("p j (h c) -> p (j h) c", c=HD), ALU.add).then_inc(v_ready, 1)

            dve.sem_inc(v_ready, 2)
            dve.wait_ge(consts, 16 * 7)
            dve.wait_ge(ones, 2)
            normalise(0, 0, 0)
            dve.tensor_copy(w_s[0][:], w_sb[:]).then_inc(w_high, 1)
            dve.wait_ge(w_high, 1)
            dve.tensor_tensor(w_s[1][:], w_sb[:], w_s[0][:].bitcast(F32), ALU.subtract).then_inc(w_low, 1)
            split(0, 0)
            normalise(1, 1, 0)
            with dve.Fori(0, TILES // 2 - 1) as it:
                for k in range(2):
                    tile(it * 2 + k, k, it, True, True)
            for k in range(2):
                tile(TILES - 2 + k, k, TILES // 2 - 1, k == 0, False)

        @block.tensor
        def _(pe):
            def transpose(t, k):
                pe.wait_ge(xn_ready, t * BLOCKS + BLOCKS)
                for m in range(KT):
                    for j in range(BLOCKS):
                        ins = pe.transpose(ps_T[m][:, j * P:(j + 1) * P], xn[k][:, j, m * P:(m + 1) * P], ident[:])
                    ins.then_inc(xT_psum, 1)

            def tile(t, k, after):
                pe.wait_ge(xT_low, t * KT + KT)
                for m in range(4):
                    pe.wait_ge(qk_full, t * 4 + m + 1)
                    for c in range(KT):
                        for n, (wh, xh) in enumerate(PASSES):
                            ins = pe.matmul(ps_qk[m][:], w_s[wh][:, m // 2, c, (m % 2) * P:(m % 2 + 1) * P],
                                            xnT_s[k][xh][:, c], start=c == 0 and n == 0,
                                            stop=c == KT - 1 and n == len(PASSES) - 1)
                    ins.then_inc(qk_psum, 1)
                    if m == 1 and after:
                        transpose(t + 1, 1 - k)
                for m in range(2):
                    pe.wait_ge(v_ready, t * 2 + m + 1)
                    for j in range(2):
                        for c in range(KT):
                            for n, (wh, xh) in enumerate(PASSES):
                                ins = pe.matmul(ps_v[m][:, j], xnT_s[k][xh][:, c, (2 * m + j) * P:(2 * m + j + 1) * P],
                                                w_s[wh][:, 2, c], start=c == 0 and n == 0,
                                                stop=c == KT - 1 and n == len(PASSES) - 1)
                    ins.then_inc(v_psum, 1)

            pe.wait_ge(consts, 16 * 7)
            transpose(0, 0)
            pe.wait_ge(w_low, 1)
            with pe.Fori(0, TILES // 2 - 1) as it:
                for k in range(2):
                    tile(it * 2 + k, k, True)
            tile(TILES - 2, 0, True)
            tile(TILES - 1, 1, False)


UNITS = [(j, kb, max(0, kb - BLOCKS * j) * P) for j in reversed(range(TILES_B)) for kb in range(BLOCKS * (j + 1))]
LAST = {max(u for u, x in enumerate(UNITS) if x[0] == j): j for j in range(TILES_B)}
NU = len(UNITS)
AHEAD = 2
RING = 4
QB = S // P
LATER = 4
EXTRA = 16
BANKS = 3
KMAX = P - 2
KSCORE = P


def max_items():
    items = []
    for j in reversed(range(TILES_B)):
        for h in range(0, G, 2):
            for head in (h, h + 1):
                items.append(("chunk", j, j, [(head, 3, 0, 4 * P)]))
                items.append(("chunk", j, j, [(head, 2, 0, 3 * P), (head, 0, 3 * P, P)]))
            pair = [(h, 1, 0, 2 * P), (h + 1, 1, 2 * P, 2 * P)]
            items += [("chunk", j, j, [x]) for x in pair] if (j, h) == (0, 0) else [("chunk", j, j, pair)]
        for c in reversed(range(j)):
            items += [("chunk", j, c, [(h, i, 0, TILE)]) for i in range(BLOCKS) for h in range(G)]
    for j in range(TILES_B):
        last = max(y for y, x in enumerate(items) if x[0] == "chunk" and x[1] == j)
        items.insert(min(last + 1 + LATER, len(items)), ("rows", j))
    return items


ITEMS = max_items()
NI = len(ITEMS)
EARLY = ITEMS.index(("rows", TILES_B - 1)) + 1 + EXTRA
LAST_CHUNK = {max(y for y, x in enumerate(ITEMS) if x[0] == "chunk" and x[1] == j): j for j in range(TILES_B)}
assert NI % BANKS == 0
RECIPROCALS = 20


def item_plan():
    items = [(0, y) for y in range(EARLY, NI)] + [(1, y) for y in range(EARLY)]

    def vector_time(y):
        return 900 if ITEMS[y][0] == "rows" else TILE + 120

    pieces = [TILE - first + P for _, _, first in UNITS for _ in range(3)]
    whole, plan, at, done, spent = sum(vector_time(y) for _, y in items), [], 0, 0, 0
    for w in pieces:
        at += w
        piece = []
        while done < len(items) and spent <= whole * at / sum(pieces):
            piece.append(items[done])
            spent += vector_time(items[done][1])
            done += 1
        plan.append(piece)
    assert done == len(items)
    return plan


class Beginning:

    def __init__(self, nc, ctx, x_in, num_all, rec_all, wo, bo, wr, temperature, experts):
        def sb(name, shape):
            return ctx.enter_context(nc.sbuf_tensor("be_" + name, shape, F32))

        def sem(name):
            return ctx.enter_context(nc.semaphore("be_" + name))

        self.x_in, self.num_all, self.rec_all = x_in, num_all, rec_all
        self.wo, self.bo, self.wr, self.temperature, self.experts = wo, bo, wr, temperature, experts
        self.wo_sb = sb("wo", [P, KT, D])
        self.bo_row = sb("bo", [P, D])
        self.wr_sb = sb("wr", [P, KT, E])
        self.temp = sb("temp", [P, 1])
        self.num = sb("num", [P, KT, TILE])
        self.rec = sb("rec", [P, KT, TILE])
        self.x_t = sb("x", [P, BLOCKS, D])
        self.stage = sb("stage", [P, 3, KT, I])
        self.consts = sem("consts_landed")
        self.x_landed, self.num_landed = sem("x_landed"), sem("num_landed")
        self.rec_landed = sem("rec_landed")
        self.staged = sem("staged")

    def load_tile(self, sp, b, i, t):
        for h in range(H):
            row = (h * HD) % P
            sp.dma_start(self.rec[row:row + HD, h * HD // P, :],
                         self.rec_all[bass.ds(b * H + h, 1), i * TILE:(i + 1) * TILE].to_broadcast([HD, TILE])).then_inc(self.rec_landed, 16)
        sp.dma_start(self.num[:], self.num_all[bass.ds(b * D, D), i * TILE:(i + 1) * TILE].rearrange(
            "(c p) n -> p c n", p=P)).then_inc(self.num_landed, 16)
        sp.dma_start(self.x_t[:], self.x_in[bass.ds(t * TILE, TILE), :].rearrange("(j p) d -> p j d", p=P)).then_inc(self.x_landed, 16)

    def load_expert(self, sp, e, stage, staged):
        for n, matrix in enumerate(self.experts):
            sp.dma_start(stage[:, n], matrix[e].rearrange("(c p) i -> p c i", p=P)).then_inc(staged, 16)

    def load(self, sp):
        sp.dma_start(self.wo_sb[:], self.wo.rearrange("(k p) n -> p k n", p=P)).then_inc(self.consts, 16)
        sp.dma_start(self.bo_row[:], self.bo.rearrange("(a n) -> a n", a=1).to_broadcast([P, D])).then_inc(self.consts, 16)
        sp.dma_start(self.wr_sb[:], self.wr.rearrange("(k p) n -> p k n", p=P)).then_inc(self.consts, 16)
        sp.dma_start(self.temp[:], self.temperature.rearrange("(a n) -> a n", a=1).to_broadcast([P, 1])).then_inc(self.consts, 16)
        self.load_tile(sp, 0, 0, 0)
        self.load_expert(sp, 0, self.stage, self.staged)


def sums(dram, n):
    return dram[bass.ds(n * G, G), :].rearrange("h (a n) -> (h a) n", n=G * S // P)


def attend(nc, ident, q_hi, q_lo, k_hi, k_lo, v_all, m_all, num_all, den_all, rec_all, beginning):
    with ExitStack() as ctx:
        def sb(name, shape, dt=F32):
            return ctx.enter_context(nc.sbuf_tensor("at_" + name, shape, dt))

        def sem(name):
            return ctx.enter_context(nc.semaphore("at_" + name))

        q_st = [sb(f"q{k}", [KSCORE, G, S], F32R) for k in range(2)]
        k_st = [sb(f"k{k}", [KSCORE, G, S], F32R) for k in range(2)]
        v_st = [sb(f"v{k}", [P, QB, G * VW]) for k in range(2)]
        probs = [sb(f"probs{r}", [P, G, TILE]) for r in range(RING)]
        mask = sb("mask", [P, P], BF16)
        ident16 = sb("ident16", [P, P], BF16)
        part = sb("part", [P, TILES_B, G, BLOCKS, TILES_B])
        row_max = sb("row_max", [P, G, BLOCKS])
        max_h = sb("max_h", [P, G * BLOCKS], F32R)
        neg_max = sb("neg_max", [P, TILES_B, 2, G * BLOCKS])
        max_rows = sb("max_rows", [P, P], F32R)
        o_sb = [sb(f"o{k}", [P, TILE]) for k in range(2)]
        den = sb("den", [P, G * S // P])
        ps_s = [ctx.enter_context(nc.psum_tensor(f"at_pss{m}", [P, 2, TILE], F32)) for m in range(2)]
        ps_m = [ctx.enter_context(nc.psum_tensor(f"at_psm{m}", [P, TILE], F32)) for m in range(BANKS)]
        ps_o = ctx.enter_context(nc.psum_tensor("at_pso", [P, TILE], F32))

        passed_pool, passed_sp = sem("passed_pool"), sem("passed_sp")
        init = sem("init")
        pool_made = sem("pool_made")
        DVE_MADE, EVEN_MADE, ALL_MADE = 4, 3, 5
        landed = [[sem(f"landed{k}{c}") for c in range(TILES_B)] for k in range(2)]
        v_landed = [sem(f"v_landed{k}") for k in range(2)]
        item_psum = sem("item_psum")
        item_done = sem("item_done")
        max_step = sem("max_step")
        rows_saved = sem("rows_saved")
        rows_landed = [sem(f"rows_landed{j}") for j in range(TILES_B)]
        score_psum = sem("score_psum")
        exp_ready = sem("exp_ready")
        masked = sem("masked")
        unit_done = sem("unit_done")
        o_ready = sem("o_ready")
        o_stored = [sem(f"o_stored{k}") for k in range(2)]
        den_landed = sem("den_landed")
        rec_ready, rec_saved = sem("rec_ready"), sem("rec_saved")

        block = ctx.enter_context(nc.Block())
        QUARTER = 8 * 16
        MAX_STEPS = 4
        STORED = 2 * G * 16

        def load_quarter(sp, n, k, c):
            cols = slice(c * TILE, (c + 1) * TILE)
            rows = bass.ds(n * (G * HD), G * HD)
            for stack, halves in ((q_st[k], (q_hi, q_hi, q_lo, q_lo)), (k_st[k], (k_hi, k_lo, k_hi, k_lo))):
                for slot, dram in enumerate(halves):
                    sp.dma_start(stack[slot * HD:(slot + 1) * HD, :, cols].bitcast(F32),
                                 dram[rows, cols].rearrange("(h r) n -> r h n", r=HD)).then_inc(landed[k][c], 16)

        def load_v(sp, n, k):
            for c in range(TILES_B):
                sp.dma_start(v_st[k][:, c * BLOCKS:(c + 1) * BLOCKS],
                             v_all[bass.ds(n, 1), c * TILE:(c + 1) * TILE, :].rearrange(
                                 "a (i p) n -> p (a i) n", p=P)).then_inc(v_landed[k], 16)

        @block.sync
        def _(sp):
            def store_maxima(n, k, j):
                nth = n * TILES_B + (TILES_B - 1 - j)
                done = n * NI + (ITEMS.index(("rows", j)) + 1)
                wait_apart(sp, item_done, done, passed_sp)
                rows = bass.ds(n * P + j * (P // TILES_B), P // TILES_B)
                sp.dma_start(m_all[rows, :], max_rows[j * (P // TILES_B):(j + 1) * (P // TILES_B)].bitcast(F32)).then_inc(rows_saved, 16)
                wait_apart(sp, rows_saved, nth * 16 + 16 * (TILES_B + 1), passed_sp)
                sp.dma_start(q_st[k][KMAX:KSCORE, :, j * TILE:(j + 1) * TILE].bitcast(F32),
                             m_all[rows, :].rearrange("(a h i) n -> a h (i n)", a=2, h=G)).then_inc(rows_landed[j], 16)

            def next_quarter(n, k, c):
                last = max(u for u, x in enumerate(UNITS) if x[0] == c)
                wait_apart(sp, score_psum, n * (2 * NU) + 2 * (last + 1), passed_sp)
                load_quarter(sp, n + 2, k, c)

            def store_output(n, j):
                wait_apart(sp, o_ready, n * TILES_B + (TILES_B - j + 1), passed_sp)
                for h in range(G):
                    sp.dma_start(num_all[bass.ds(n * (G * HD) + h * HD, HD), j * TILE:(j + 1) * TILE],
                                 o_sb[j % 2][h * VW:h * VW + HD]).then_inc(o_stored[j % 2], 16)
                    sp.dma_start(den_all[bass.ds(n * G + h, 1), j * TILE:(j + 1) * TILE],
                                 o_sb[j % 2][h * VW + HD:h * VW + HD + 1]).then_inc(o_stored[j % 2], 16)

            def load_sums(n):
                for m in range(2):
                    wait_apart(sp, o_stored[m], n * (2 * STORED) + 3 * STORED, passed_sp)
                if not isinstance(n, int) or n > 0:
                    wait_apart(sp, rec_saved, n * 16, passed_sp)
                sp.dma_start(den[:], sums(den_all, n)).then_inc(den_landed, 16)

            def store_reciprocals(n):
                wait_apart(sp, rec_ready, n + 1, passed_sp)
                sp.dma_start(sums(rec_all, n), den[:]).then_inc(rec_saved, 16)

            def group(n, k, load=True, after=True, very_first=False):
                store_maxima(n, k, 2)
                if load:
                    next_quarter(n, k, 3)
                store_output(n, 3)
                if not very_first:
                    load_sums(n - 1)
                store_maxima(n, k, 1)
                store_maxima(n, k, 0)
                if load:
                    next_quarter(n, k, 2)
                store_output(n, 2)
                if not very_first:
                    store_reciprocals(n - 1)
                if load:
                    next_quarter(n, k, 1)
                if after:
                    store_maxima(n + 1, 1 - k, 3)
                store_output(n, 1)
                if load:
                    next_quarter(n, k, 0)
                store_output(n, 0)
                if load:
                    load_v(sp, n + 2, k)

            for n in range(2):
                for c in reversed(range(TILES_B)):
                    load_quarter(sp, n, n, c)
                load_v(sp, n, n)
            sp.wait_ge(init, DVE_MADE)
            sp.wait_ge(pool_made, ALL_MADE)
            store_maxima(0, 0, 3)
            group(0, 0, very_first=True)
            group(1, 1)
            with sp.Fori(1, GROUPS // 2 - 1) as it:
                for k in range(2):
                    group(it * 2 + k, k)
            group(GROUPS - 2, 0, load=False)
            beginning.load(sp)
            group(GROUPS - 1, 1, load=False, after=False)
            sp.wait_ge(rec_saved, 16 * (GROUPS - 1))
            for k in range(2):
                sp.wait_ge(o_stored[k], STORED * (2 * GROUPS + 1))

        @block.gpsimd
        def _(pool):
            pool.memset(mask[:], 0.0).then_inc(pool_made, 1)
            pool.wait_ge(pool_made, 1)
            pool.affine_select(out=mask[:], in_=mask[:], compare_op=ALU.is_ge, fill=LOW,
                               base=0, pattern=[[-1, P]], channel_multiplier=1).then_inc(pool_made, 1)
            pool.wait_ge(pool_made, 2)
            pool.memset(k_st[0][4 * HD:, :, :].bitcast(F32), 1.0).then_inc(pool_made, 1)
            pool.wait_ge(pool_made, EVEN_MADE)
            pool.memset(q_st[1][4 * HD:, :, :].bitcast(F32), 0.0).then_inc(pool_made, 1)
            pool.wait_ge(pool_made, EVEN_MADE + 1)
            pool.memset(k_st[1][4 * HD:, :, :].bitcast(F32), 1.0).then_inc(pool_made, 1)
            pool.wait_ge(pool_made, ALL_MADE)
            with pool.Fori(0, GROUPS) as n:
                for u, (j, kb, first) in enumerate(UNITS):
                    if kb < BLOCKS * j:
                        continue
                    wait_apart(pool, exp_ready, n * (2 * NU) + 2 * (u + 1), passed_pool)
                    diagonal = probs[u % RING][:, :, first:first + P]
                    pool.affine_select(out=diagonal, in_=diagonal, compare_op=ALU.is_ge, fill=0.0, base=0,
                                       pattern=[[0, G], [1, P]], channel_multiplier=-1).then_inc(masked, 1)

        @block.scalar
        def _(act):
            def exponentials(n, u):
                _, _, first = UNITS[u]
                for half in range(2):
                    act.wait_ge(score_psum, n * (2 * NU) + 2 * u + half + 1)
                    act.activation(probs[u % RING][:, 2 * half:2 * half + 2, first:], ps_s[half][:, :, first:],
                                   ACT.Exp, scale=HD ** -0.5).then_inc(exp_ready, 1)

            def group(n, after=True):
                for u in range(NU):
                    if u + AHEAD < NU:
                        exponentials(n, u + AHEAD)
                    elif after:
                        exponentials(n + 1, u + AHEAD - NU)
                    if u in LAST:
                        j = LAST[u]
                        act.wait_ge(unit_done, n * NU + u + 1)
                        act.wait_ge(o_stored[j % 2], n * (2 * STORED) + STORED * ((TILES_B - 1 - j) // 2 + 1))
                        act.activation(o_sb[j % 2][:], ps_o[:], ACT.Copy).then_inc(o_ready, 1)

            act.sem_inc(o_ready, 1)
            for k in range(2):
                act.sem_inc(o_stored[k], STORED)
            for u in range(AHEAD):
                exponentials(0, u)
            with act.Fori(0, GROUPS - 1) as n:
                group(n)
            group(GROUPS - 1, after=False)

        @block.vector
        def _(dve):
            dve.sem_inc(rows_saved, 16 * TILES_B)
            dve.memset(neg_max[:], 0.0).then_inc(init, 1)
            dve.memset(part[:], LOW).then_inc(init, 1)
            dve.tensor_copy(ident16[:], ident[:]).then_inc(init, 1)
            dve.memset(q_st[0][4 * HD:, :, :].bitcast(F32), 0.0).then_inc(init, 1)
            dve.wait_ge(init, DVE_MADE)

            def turn_over(n):
                dve.wait_ge(den_landed, n * 16 + 16)
                dve.reciprocal(den[:], den[:]).then_inc(rec_ready, 1)

            def group(n, reciprocals=True):
                for y, item in enumerate(ITEMS):
                    if y == RECIPROCALS and reciprocals:
                        turn_over(n - 2)
                    if item[0] == "rows":
                        j = item[1]
                        rows = slice(j * (P // TILES_B), (j + 1) * (P // TILES_B))
                        dve.wait_ge(rows_saved, n * (16 * TILES_B) + 16 * (TILES_B - j))
                        dve.wait_ge(item_psum, n * NI + y + 1)
                        dve.tensor_copy(max_rows[rows], ps_m[y % BANKS][rows, 0:P]).then_inc(item_done, 1)
                        continue
                    _, j, c, segments = item
                    dve.wait_ge(item_psum, n * NI + y + 1)
                    _, i, first, width = segments[0]
                    if width == segments[-1][3]:
                        h = segments[0][0]
                        dve.tensor_reduce(part[:, j, h:h + len(segments), i, c], ps_m[y % BANKS][:, first:first + len(segments) * width].rearrange(
                            "p (a n) -> p a n", n=width), AX_X, ALU.max).then_inc(item_done, 1)
                    else:
                        for h, i, first, width in segments:
                            ins = dve.tensor_reduce(part[:, j, h, i, c:c + 1], ps_m[y % BANKS][:, first:first + width], AX_X, ALU.max)
                        ins.then_inc(item_done, 1)
                    if y not in LAST_CHUNK:
                        continue
                    steps = n * (TILES_B * MAX_STEPS) + (TILES_B - 1 - j) * MAX_STEPS
                    dve.wait_ge(item_done, n * NI + y + 1)
                    dve.tensor_reduce(row_max[:].rearrange("p h i -> p (h i)"), part[:, j].rearrange("p h i c -> p (h i) c"), AX_X, ALU.max).then_inc(max_step, 1)
                    dve.wait_ge(max_step, steps + 1)
                    row = row_max[:].rearrange("p h i -> p (h i)")
                    dve.tensor_scalar(max_h[:], row, -1.0, None, ALU.mult).then_inc(max_step, 1)
                    dve.wait_ge(max_step, steps + 2)
                    dve.tensor_copy(neg_max[:, j, 0], max_h[:].bitcast(F32)).then_inc(max_step, 1)
                    dve.scalar_tensor_tensor(out=neg_max[:, j, 1], in0=row, scalar=-1.0, in1=max_h[:].bitcast(F32),
                                             op0=ALU.mult, op1=ALU.subtract).then_inc(max_step, 1)

            for n in range(2):
                group(n, reciprocals=False)
            with dve.Fori(2, GROUPS) as n:
                group(n)
            turn_over(GROUPS - 2)

        @block.tensor
        def _(pe):
            def scores(n, k, u, half, very_first=False):
                j, kb, first = UNITS[u]
                if kb == 0 and half == 0:
                    pe.wait_ge(rows_landed[j], n * 16 + 16)
                if not very_first:
                    pe.wait_ge(exp_ready, n * (2 * NU) + (2 * u - 1 + half))
                for h in (2 * half, 2 * half + 1):
                    ins = pe.matmul(ps_s[half][:, h % 2, first:], k_st[k][:, h, kb * P:(kb + 1) * P],
                                    q_st[k][:, h, j * TILE + first:(j + 1) * TILE], start=True, stop=True)
                ins.then_inc(score_psum, 1)

            def item(n, k, pair, y):
                if y >= BANKS or not (isinstance(n, int) and n == 0):
                    pe.wait_ge(item_done, n * NI + (y - BANKS + 1))
                if ITEMS[y][0] == "rows":
                    j = ITEMS[y][1]
                    pe.wait_ge(max_step, n * (TILES_B * MAX_STEPS) + (TILES_B - j) * MAX_STEPS)
                    pe.transpose(ps_m[y % BANKS][:, 0:P], neg_max[:].rearrange("p j a n -> p (j a n)"), ident[:]).then_inc(item_psum, 1)
                    return
                _, j, c, segments = ITEMS[y]
                if j == TILES_B - 1 and segments[0][:2] == ((0, 3) if c == j else (0, 0)):
                    pe.wait_ge(landed[k][c], pair * QUARTER + QUARTER)
                for h, i, first, width in segments:
                    query = (j * BLOCKS + i) * P
                    ins = pe.matmul(ps_m[y % BANKS][:, first:first + width], q_st[k][0:KMAX, h, query:query + P],
                                    k_st[k][0:KMAX, h, c * TILE:c * TILE + width], start=True, stop=c < j)
                    if c == j:
                        ins = pe.matmul(ps_m[y % BANKS][:, first + width - P:first + width], ident16[:], mask[:],
                                        start=False, stop=True)
                ins.then_inc(item_psum, 1)

            def times_v(n, k, pair, u):
                j, kb, first = UNITS[u]
                if u == 0:
                    pe.wait_ge(v_landed[k], pair * (16 * TILES_B) + 16 * TILES_B)
                if kb == 0:
                    pe.wait_ge(o_ready, n * TILES_B + (TILES_B - j))
                if kb >= BLOCKS * j:
                    pe.wait_ge(masked, n * (TILES_B * BLOCKS) + (TILES_B - 1 - j) * BLOCKS + kb - BLOCKS * j + 1)
                else:
                    pe.wait_ge(exp_ready, n * (2 * NU) + 2 * (u + 1))
                for h in range(G):
                    ins = pe.matmul(ps_o[h * VW:(h + 1) * VW, first:], v_st[k][:, kb, h * VW:(h + 1) * VW],
                                    probs[u % RING][:, h, first:], start=kb == 0, stop=u in LAST)
                ins.then_inc(unit_done, 1)

            plan = item_plan()

            def group(n, k, pair, after=True):
                if k == 0:
                    pe.wait_ge(pool_made, ALL_MADE)
                for u in range(NU):
                    for piece in range(3):
                        if piece == 2:
                            times_v(n, k, pair, u)
                        elif u + AHEAD < NU:
                            scores(n, k, u + AHEAD, piece)
                        elif after:
                            scores(n + 1, 1 - k, u + AHEAD - NU, piece)
                        for later, y in plan[3 * u + piece]:
                            if not later:
                                item(n, k, pair, y)
                            elif after:
                                item(n + 1, 1 - k, pair + k, y)

            pe.wait_ge(init, DVE_MADE)
            pe.wait_ge(pool_made, EVEN_MADE)
            for y in range(EARLY):
                item(0, 0, 0, y)
            for u in range(AHEAD):
                for half in range(2):
                    scores(0, 0, u, half, very_first=u == 0)
            with pe.Fori(0, GROUPS // 2 - 1) as it:
                for k in range(2):
                    group(it * 2 + k, k, it)
            group(GROUPS - 2, 0, GROUPS // 2 - 1)
            group(GROUPS - 1, 1, GROUPS // 2 - 1, after=False)


CENTER = 1.0 / math.e
LOWER = 0.5 - math.log(4.0 / 3.0)
UPPER = 0.5
SLICES = E * I // P
SE = SLICES // E
STAGES = 4
HRING = 2 * SE
WEIGH_STEPS = 35


def feed(nc, ident, beginning, den_all, rec_all, out):
    with ExitStack() as ctx:
        def sb(name, shape, dt=F32):
            return ctx.enter_context(nc.sbuf_tensor("fe_" + name, shape, dt))

        def sem(name):
            return ctx.enter_context(nc.semaphore("fe_" + name))

        def ps(name, shape):
            return ctx.enter_context(nc.psum_tensor("fe_ps" + name, shape, F32))

        wo_sb, bo_row, wr_sb, temp = beginning.wo_sb, beginning.bo_row, beginning.wr_sb, beginning.temp
        num, rec, x_t = beginning.num, beginning.rec, beginning.x_t
        temp_r = sb("temp_r", [P, 1])
        stage = [beginning.stage] + [sb(f"stage{n}", [P, 3, KT, I]) for n in range(1, STAGES)]
        w_ex = [sb(f"w_ex{n}", [P, E, 3, KT, I], F32R) for n in range(2)]
        den = sb("den", [P, G * S // P])
        x1 = [sb(f"x1{k}", [P, BLOCKS, D]) for k in range(2)]
        stats = sb("stats", [P, BLOCKS, 6])
        moments = sb("moments", [P, BLOCKS, 2])
        small = sb("small", [P, 4, BLOCKS])
        x2 = sb("x2", [P, BLOCKS, D])
        x2_f = sb("x2f", [P, KT, TILE])
        x2_s = [[sb(f"x2s{k}{n}", [P, KT, TILE], F32R) for n in range(2)] for k in range(2)]
        z, den1, inh, zone, dist, fb, rest, top1, top2, order = (
            sb(name, [P, BLOCKS, E]) for name in "z den1 inh zone dist fb rest top1 top2 order".split())
        total, none = sb("total", [P, BLOCKS]), sb("none", [P, BLOCKS])
        w = [sb(f"w{k}", [P, BLOCKS, E]) for k in range(2)]
        silu = [sb(f"silu{k}", [P, TILE]) for k in range(2)]
        h_f = [sb(f"h_f{k}", [P, TILE]) for k in range(2)]
        h_s = [[sb(f"h{r}{n}", [P, TILE], F32R) for n in range(2)] for r in range(HRING)]
        ps_x = [ps(f"x{m}", [P, TILE]) for m in range(2)]
        ps_g = [ps(f"g{m}", [P, TILE]) for m in range(2)]
        ps_u = [ps(f"u{m}", [P, TILE]) for m in range(2)]
        ps_d = [ps(f"d{m}", [P, 2, D]) for m in range(2)]
        logits = ps_x[0][:, 0:BLOCKS * E].rearrange("p (j e) -> p j e", e=E)

        consts = beginning.consts
        staged = [beginning.staged] + [sem(f"staged{n}") for n in range(1, STAGES)]
        high_ready = sem("high_ready")
        low_ready = sem("low_ready")
        x_landed, num_landed, rec_landed = beginning.x_landed, beginning.num_landed, beginning.rec_landed
        den_landed = sem("den_landed")
        rec_ready = sem("rec_ready")
        rec_saved = sem("rec_saved")
        att_ready = sem("att_ready")
        xb_ready = sem("xb_ready")
        y_psum = sem("y_psum")
        x1_ready = sem("x1_ready")
        chain_sem = sem("ln_chain")
        passed, passed_pool, passed_sp = sem("passed"), sem("passed_pool"), sem("passed_sp")
        var_ready, std_ready, x2_ready = sem("var_ready"), sem("std_ready"), sem("x2_ready")
        xT_psum = sem("xT_psum")
        xT_ready = sem("xT_ready")
        x2_split = sem("x2_split")
        r_psum = sem("r_psum")
        step_sem = sem("step")
        z_ready, exps = sem("z_ready"), sem("exps")
        w_ready = sem("w_ready")
        gu_psum = sem("gu_psum")
        silu_ready = sem("silu_ready")
        h_ready = sem("h_ready")
        h_high = sem("h_high")
        h_low = sem("h_low")
        down_psum = sem("down_psum")
        added = sem("added")
        out_stored = [sem(f"out_stored{k}") for k in range(2)]

        block = ctx.enter_context(nc.Block())

        PAIRS = TILES // 2 - 1

        @block.sync
        def _(sp):
            def load(b, i, t):
                sp.wait_ge(x1_ready, t * 2)
                sp.wait_ge(y_psum, t * 2)
                beginning.load_tile(sp, b, i, t)

            def store(t, k):
                sp.wait_ge(added, t * (2 * E) + 2 * E)
                sp.dma_start(out[bass.ds(t * TILE, TILE), :].rearrange("(j p) d -> p j d", p=P), x1[k][:]).then_inc(out_stored[k], 16)

            sp.dma_start(den[:], sums(den_all, GROUPS - 1)).then_inc(den_landed, 16)
            for e in range(1, E):
                if e >= STAGES:
                    sp.wait_ge(low_ready, e - STAGES + 1)
                beginning.load_expert(sp, e, stage[e % STAGES], staged[e % STAGES])
            sp.wait_ge(rec_ready, 1)
            sp.dma_start(sums(rec_all, GROUPS - 1), den[:]).then_inc(rec_saved, 16)
            sp.wait_ge(rec_saved, 16)
            for t in range(1, TILES_B):
                load(0, t, t)
                if t >= 2:
                    store(t - 2, t % 2)
            with sp.Fori(1, B) as b:
                for i in range(TILES_B):
                    t = b * TILES_B + i
                    load(b, i, t)
                    store(t - 2, i % 2)
            for t in (TILES - 2, TILES - 1):
                store(t, t % 2)
            for k in range(2):
                sp.wait_ge(out_stored[k], 16 * (TILES // 2))

        @block.gpsimd
        def _(pool):
            def divided(t):
                pool.wait_ge(x_landed, t * 16 + 16)
                pool.tensor_tensor(x_t[:], x_t[:], bo_row[:].unsqueeze(1).to_broadcast([P, BLOCKS, D]),
                                   ALU.add).then_inc(xb_ready, 1)
                pool.wait_ge(num_landed, t * 16 + 16)
                pool.wait_ge(rec_landed, t * (16 * H) + 16 * H)
                for c in range(KT):
                    pool.tensor_tensor(num[:, c], num[:, c], rec[:, c], ALU.mult).then_inc(att_ready, 1)

            def split(t, k):
                for c in range(KT):
                    wait_apart(pool, xT_ready, t * KT + c + 1, passed_pool)
                    pool.tensor_copy(x2_s[k][0][:, c], x2_f[:, c]).then_inc(x2_split, 1)
                    pool.wait_ge(x2_split, t * (2 * KT) + 2 * c + 1)
                    pool.tensor_tensor(x2_s[k][1][:, c], x2_f[:, c], x2_s[k][0][:, c].bitcast(F32), ALU.subtract).then_inc(x2_split, 1)

            def low(e):
                pool.wait_ge(high_ready, e + 1)
                pool.tensor_tensor(w_ex[1][:, e], stage[e % STAGES][:], w_ex[0][:, e].bitcast(F32), ALU.subtract).then_inc(low_ready, 1)

            pool.wait_ge(consts, 16 * 4)
            divided(0)
            low(0)
            low(1)
            split(0, 0)
            for e in range(2, E):
                low(e)
            divided(1)
            split(1, 1)
            with pool.Fori(0, PAIRS) as it:
                for k in range(2):
                    t = it * 2 + (k + 2)
                    divided(t)
                    split(t, k)

        @block.scalar
        def _(act):
            def high(e):
                act.wait_ge(staged[e % STAGES], 48 * (e // STAGES + 1))
                act.activation(w_ex[0][:, e], stage[e % STAGES][:], ACT.Copy).then_inc(high_ready, 1)

            def root(t):
                act.wait_ge(var_ready, t + 1)
                act.activation(small[:, 1, :], small[:, 0, :], ACT.Sqrt).then_inc(std_ready, 1)

            def transposed(t):
                for m in range(KT):
                    act.wait_ge(xT_psum, t * KT + m + 1)
                    act.activation(x2_f[:, m], ps_x[m][:], ACT.Copy).then_inc(xT_ready, 1)

            def exp_z(t):
                act.wait_ge(z_ready, t * 2 + 1)
                act.activation(den1[:], z[:], ACT.Exp, scale=-1.0).then_inc(exps, 1)

            def exp_dist(t, k):
                act.wait_ge(z_ready, t * 2 + 2)
                act.activation(w[k][:], dist[:], ACT.Exp, scale=-1.0 / 0.1).then_inc(exps, 1)
                act.activation(fb[:], dist[:], ACT.Exp, scale=-1.0 / 0.3).then_inc(exps, 1)

            def tile(t, k, very_first=False, after=True):
                for s in range(SLICES):
                    act.wait_ge(gu_psum, t * SLICES + s + 1)
                    act.activation(silu[s % 2][:], ps_g[s % 2][:], ACT.Silu).then_inc(silu_ready, 1)
                    if very_first and s < E - STAGES:
                        high(s + STAGES)
                    if not after:
                        continue
                    if s == 8:
                        root(t + 1)
                    if s == 11:
                        transposed(t + 1)
                    if s == 14:
                        exp_z(t + 1)
                    if s == 15:
                        exp_dist(t + 1, 1 - k)

            root(0)
            high(0)
            high(1)
            transposed(0)
            exp_z(0)
            exp_dist(0, 0)
            high(2)
            high(3)
            tile(0, 0, very_first=True)
            with act.Fori(0, PAIRS) as it:
                for k in range(2):
                    tile(it * 2 + (k + 1), 1 - k)
            tile(TILES - 1, 1, after=False)

        @block.vector
        def _(dve):
            chain = Tally(chain_sem, LN_CHAIN)
            step = Tally(step_sem, WEIGH_STEPS)
            tt, ts = dve.tensor_tensor, dve.tensor_scalar

            def do(t, instruction):
                step.up(instruction)
                step.wait(dve, t)

            def over(column):
                return column.unsqueeze(2).to_broadcast([P, BLOCKS, E])

            def residual(t, k, stored):
                dve.wait_ge(xb_ready, t + 1)
                if stored is not None:
                    dve.wait_ge(out_stored[k], stored * 16)
                for m in range(2):
                    dve.wait_ge(y_psum, t * 2 + m + 1)
                    tt(x1[k][:, 2 * m:2 * m + 2], ps_x[m][:].rearrange("p (j d) -> p j d", d=D),
                       x_t[:, 2 * m:2 * m + 2], ALU.add).then_inc(x1_ready, 1)

            def logits_out(t):
                dve.wait_ge(r_psum, t + 1)
                ts(z[:], logits, temp_r[:, 0:1], None, ALU.mult).then_inc(z_ready, 1)

            def distance(t):
                step.start()
                dve.wait_ge(exps, t * 3 + 1)
                do(t, ts(den1[:], den1[:], 1.0, None, ALU.add))
                do(t, dve.reciprocal(inh[:], den1[:]))
                do(t, ts(zone[:], inh[:], LOWER, None, ALU.is_ge))
                do(t, dve.scalar_tensor_tensor(out=zone[:], in0=inh[:], scalar=UPPER, in1=zone[:], op0=ALU.is_le, op1=ALU.mult))
                do(t, ts(inh[:], inh[:], CENTER, None, ALU.subtract))
                dve.scalar_tensor_tensor(out=dist[:], in0=inh[:], scalar=-1.0, in1=inh[:], op0=ALU.mult, op1=ALU.max).then_inc(z_ready, 1)

            def largest(t, mask):
                do(t, dve.tensor_reduce(total[:], rest[:], AX_X, ALU.max))
                do(t, tt(mask[:], rest[:], over(total[:]), ALU.is_equal))
                do(t, tt(mask[:], mask[:], order[:], ALU.mult))
                do(t, dve.tensor_reduce(total[:], mask[:], AX_X, ALU.max))
                do(t, tt(mask[:], mask[:], over(total[:]), ALU.is_equal))
                do(t, dve.scalar_tensor_tensor(out=rest[:], in0=mask[:], scalar=-10.0, in1=rest[:], op0=ALU.mult, op1=ALU.add))

            def zone_weights(t, k):
                dve.wait_ge(exps, t * 3 + 3)
                do(t, tt(w[k][:], w[k][:], zone[:], ALU.mult))
                do(t, dve.tensor_reduce(total[:], w[k][:], AX_X, ALU.add))
                do(t, ts(none[:], total[:], 1e-8, None, ALU.is_lt))
                do(t, dve.tensor_copy(rest[:], fb[:]))
                largest(t, top1)

            def fallback(t):
                largest(t, top2)
                do(t, tt(top1[:], top1[:], top2[:], ALU.add))
                do(t, tt(fb[:], fb[:], top1[:], ALU.mult))

            def normalise(t, x):
                do(t, dve.tensor_reduce(total[:], x[:], AX_X, ALU.add))
                do(t, ts(total[:], total[:], 1e-8, None, ALU.max))
                do(t, dve.reciprocal(total[:], total[:]))
                do(t, tt(x[:], x[:], over(total[:]), ALU.mult))

            def weights(t, k):
                normalise(t, fb)
                do(t, tt(fb[:], fb[:], over(none[:]), ALU.mult))
                do(t, ts(none[:], none[:], -1.0, 1.0, ALU.mult, ALU.add))
                do(t, tt(w[k][:], w[k][:], over(none[:]), ALU.mult))
                do(t, tt(w[k][:], w[k][:], fb[:], ALU.add))
                normalise(t, w[k])
                step.end()

            def hidden(t, s, very_first):
                g, r = t * SLICES + s, s % HRING
                if not (very_first and s < 2):
                    dve.wait_ge(h_low, g - 1)
                dve.wait_ge(silu_ready, g + 1)
                tt(h_f[s % 2][:], ps_u[s % 2][:], silu[s % 2][:], ALU.mult).then_inc(h_ready, 1)
                dve.wait_ge(h_ready, g + 1)
                if s % SE == 0 and not (very_first and s < HRING):
                    dve.wait_ge(down_psum, t * (2 * E) + (s // SE - 1) * 2)
                dve.tensor_copy(h_s[r][0][:], h_f[s % 2][:]).then_inc(h_high, 1)
                dve.wait_ge(h_high, g + 1)
                tt(h_s[r][1][:], h_f[s % 2][:], h_s[r][0][:].bitcast(F32), ALU.subtract).then_inc(h_low, 1)

            def add_expert(t, k, e, very_first=False):
                for m in range(2):
                    dve.wait_ge(down_psum, t * (2 * E) + 2 * e + m + 1)
                    if not (very_first and e == 0):
                        dve.wait_ge(added, t * (2 * E) + 2 * e + m - 1)
                    for j in (2 * m, 2 * m + 1):
                        ins = dve.scalar_tensor_tensor(out=x1[k][:, j], in0=ps_d[m][:, j % 2], scalar=w[k][:, j, e:e + 1],
                                                       in1=x1[k][:, j], op0=ALU.mult, op1=ALU.add)
                    ins.then_inc(added, 1)

            def tile(t, k, stored, very_first=False, after=True):
                for s in range(SLICES):
                    hidden(t, s, very_first)
                    if s == 1 and not very_first:
                        add_expert(t - 1, 1 - k, E - 1)
                    if s >= 3 and s % 2 == 1:
                        add_expert(t, k, (s - 3) // 2, very_first)
                    if s == 0:
                        fallback(t)
                    if s == 2:
                        weights(t, k)
                    if not after:
                        continue
                    if s == 6:
                        residual(t + 1, 1 - k, stored)
                    if s == 7:
                        dve.wait_ge(x1_ready, t * 2 + 4)
                        chain.start()
                        ln_variance(dve, chain, t + 1, passed, x1[1 - k], stats, moments, small, var_ready)
                    if s == 8:
                        ln_root(dve, chain, t + 1, small, var_ready, std_ready)
                        chain.end()
                        ln_scale(dve, x1[1 - k], moments, small, x2, x2_ready)
                    if s == 13:
                        logits_out(t + 1)
                    if s == 14:
                        distance(t + 1)
                    if s == 15:
                        zone_weights(t + 1, 1 - k)

            dve.wait_ge(consts, 16 * 4)
            dve.reciprocal(temp_r[:], temp[:]).then_inc(w_ready, 1)
            for e in range(E):
                dve.memset(order[:, :, e], float(E - e)).then_inc(w_ready, 1)
            dve.wait_ge(w_ready, E + 1)
            residual(0, 0, None)
            dve.wait_ge(x1_ready, 2)
            chain.start()
            ln_variance(dve, chain, 0, passed, x1[0], stats, moments, small, var_ready)
            ln_root(dve, chain, 0, small, var_ready, std_ready)
            chain.end()
            ln_scale(dve, x1[0], moments, small, x2, x2_ready)
            logits_out(0)
            distance(0)
            zone_weights(0, 0)
            dve.wait_ge(den_landed, 16)
            dve.reciprocal(den[:], den[:]).then_inc(rec_ready, 1)
            tile(0, 0, None, very_first=True)
            with dve.Fori(0, PAIRS) as it:
                for k in range(2):
                    tile(it * 2 + (k + 1), 1 - k, it + 1)
            tile(TILES - 1, 1, None, after=False)
            add_expert(TILES - 1, 1, E - 1)

        @block.tensor
        def _(pe):
            def project_out(t):
                if not isinstance(t, int) or t > 0:
                    pe.wait_ge(z_ready, t * 2 - 1)
                pe.wait_ge(att_ready, t * KT + KT)
                for m in range(2):
                    for j in range(2):
                        first = (2 * m + j) * P
                        for c in range(KT):
                            ins = pe.matmul(ps_x[m][:, j * D:(j + 1) * D], num[:, c, first:first + P], wo_sb[:, c],
                                            start=c == 0, stop=c == KT - 1)
                    ins.then_inc(y_psum, 1)

            def transpose(t):
                pe.wait_ge(x2_ready, t * BLOCKS + BLOCKS)
                for m in range(KT):
                    for j in range(BLOCKS):
                        ins = pe.transpose(ps_x[m][:, j * P:(j + 1) * P], x2[:, j, m * P:(m + 1) * P], ident[:])
                    ins.then_inc(xT_psum, 1)

            def router(t):
                pe.wait_ge(xT_ready, t * KT + KT)
                for j in range(BLOCKS):
                    for c in range(KT):
                        ins = pe.matmul(logits[:, j], x2_f[:, c, j * P:(j + 1) * P], wr_sb[:, c],
                                        start=c == 0, stop=c == KT - 1)
                ins.then_inc(r_psum, 1)

            def gate_up(t, k, s, very_first=False):
                e, i = s // SE, (s % SE) * P
                if s == 0:
                    pe.wait_ge(x2_split, t * (2 * KT) + 2 * KT)
                if very_first and s % SE == 0:
                    pe.wait_ge(low_ready, e + 1)
                if not (very_first and s < 2):
                    pe.wait_ge(h_ready, t * SLICES + (s - 1))
                for bank, matrix in ((ps_g[s % 2], 0), (ps_u[s % 2], 1)):
                    for c in range(KT):
                        for n, (wh, xh) in enumerate(PASSES):
                            ins = pe.matmul(bank[:], w_ex[wh][:, e, matrix, c, i:i + P], x2_s[k][xh][:, c],
                                            start=c == 0 and n == 0, stop=c == KT - 1 and n == len(PASSES) - 1)
                ins.then_inc(gu_psum, 1)

            def down(t, e, very_first):
                pe.wait_ge(h_low, t * SLICES + SE * (e + 1))
                for m in range(2):
                    if not (very_first and e == 0):
                        pe.wait_ge(added, t * (2 * E) + 2 * e + m - 1)
                    for j in (2 * m, 2 * m + 1):
                        for s in range(SE):
                            for n, (wh, hh) in enumerate(PASSES):
                                ins = pe.matmul(ps_d[m][:, j % 2], h_s[(e * SE + s) % HRING][hh][:, j * P:(j + 1) * P],
                                                w_ex[wh][:, e, 2, s], start=s == 0 and n == 0,
                                                stop=s == SE - 1 and n == len(PASSES) - 1)
                    ins.then_inc(down_psum, 1)

            def tile(t, k, very_first=False, after=True):
                for e in range(E):
                    for s in range(SE * (e + 1), SE * (e + 2)):
                        if s < SLICES:
                            gate_up(t, k, s, very_first)
                        elif after:
                            gate_up(t + 1, 1 - k, s - SLICES)
                    if after and e == 1:
                        project_out(t + 1)
                    if after and e == 4:
                        transpose(t + 1)
                    if after and e == 5:
                        router(t + 1)
                    down(t, e, very_first)

            pe.wait_ge(consts, 16 * 4)
            project_out(0)
            transpose(0)
            router(0)
            for s in range(SE):
                gate_up(0, 0, s, very_first=True)
            tile(0, 0, very_first=True)
            with pe.Fori(0, PAIRS) as it:
                for k in range(2):
                    tile(it * 2 + (k + 1), 1 - k)
            tile(TILES - 1, 1, after=False)


def build(nc, x, wq, bq, wk, bk, wv, bv, wo, bo, wg, wu, wd, wr, temperature, out):
    def scratch(name, shape):
        return nc.dram_tensor(name, shape, F32, kind="Internal").ap()

    q_hi, q_lo, k_hi, k_lo = (scratch(name, (B * D, S)) for name in ("q_hi", "q_lo", "k_hi", "k_lo"))
    v_all = scratch("v_all", (B * GROUPS_B, S, G * VW))
    num_all = scratch("num_all", (B * D, S))
    den_all, rec_all = (scratch(name, (B * H, S)) for name in ("den_all", "rec_all"))
    m_all = scratch("m_all", (GROUPS * P, P))
    x_in, y_out = x.rearrange("b s d -> (b s) d"), out.rearrange("b s d -> (b s) d")
    with ExitStack() as ctx:
        ident = ctx.enter_context(nc.sbuf_tensor("ident", [P, P], F32))
        made = ctx.enter_context(nc.semaphore("ident_made"))
        with nc.Block() as block:
            @block.gpsimd
            def _(pool):
                pool.memset(ident[:], 0.0).then_inc(made, 1)
                pool.wait_ge(made, 1)
                pool.affine_select(out=ident[:], in_=ident[:], compare_op=ALU.not_equal, fill=1.0, base=0,
                                   pattern=[[-1, P]], channel_multiplier=1).then_inc(made, 1)
                pool.wait_ge(made, 2)
        project(nc, ident, x_in, wq, bq, wk, bk, wv, bv, q_hi, q_lo, k_hi, k_lo, v_all)
        beginning = Beginning(nc, ctx, x_in, num_all, rec_all, wo, bo, wr, temperature, (wg, wu, wd))
        attend(nc, ident, q_hi, q_lo, k_hi, k_lo, v_all, m_all, num_all, den_all, rec_all, beginning)
        feed(nc, ident, beginning, den_all, rec_all, y_out)


_INS = ["L0_attn_x", "L0_attn_wq", "L0_attn_bq", "L0_attn_wk", "L0_attn_bk", "L0_attn_wv", "L0_attn_bv",
        "L0_attn_wo", "L0_attn_bo", "L0_ffn_Wg", "L0_ffn_Wu", "L0_ffn_Wd", "L0_ffn_Wr", "L0_ffn_temperature"]


def kernel(**inputs):
    import numpy as _np
    import concourse.bacc as _bacc
    from concourse import mybir as _mybir
    from concourse.bass_utils import run_bass_kernel_spmd as _run

    nc = _bacc.Bacc("TRN2", target_bir_lowering=False, num_devices=1)
    arrays, args = {}, []
    for name in _INS:
        a = _np.ascontiguousarray(inputs[name])
        arrays[f"in_{name}_dram"] = a
        args.append(nc.dram_tensor(f"in_{name}_dram", a.shape, _mybir.dt.from_np(a.dtype), kind="ExternalInput").ap())
    args.append(nc.dram_tensor("out_0_dram", (B, S, D), _mybir.dt.float32, kind="ExternalOutput").ap())
    build(nc, *args)
    r = _run(nc, [arrays], core_ids=[0])
    return r.results[0]["out_0_dram"]
```
